# Optimizing a Trainium2 kernel written in Bass

```python
import numpy as np
import jax
import jax.numpy as jnp

def _softmax(x, axis=-1):
    return jax.nn.softmax(x, axis=axis)

def _gelu(x):
    return jax.nn.gelu(x, approximate=True)

def _silu(x):
    return jax.nn.silu(x)

def _sigmoid(x):
    return jax.nn.sigmoid(x)

def _layernorm(x, axis=-1, eps=1e-05):
    m = jnp.mean(x, axis=axis, keepdims=True)
    v = jnp.var(x, axis=axis, keepdims=True)
    return (x - m) / jnp.sqrt(v + eps)

def _scatter_add(tgt, idx, src, axis=0):
    return tgt.at[idx].add(src)

def _segment_sum(src, seg, n):
    return jax.ops.segment_sum(src, seg, n)
kernel_name = 'mk_macaron_d1_jaxref_r8_36e828'

def setup_inputs(seed: int=0):
    np.random.seed(seed)
    _w = jnp.asarray

    def _L0_attn_setup():
        import jax, jax.numpy as jnp
        import numpy as np
        B, N, F, H = (4, 256, 128, 16)
        DH = F // H
        SQRT_D = float(DH) ** 0.5
        key = jax.random.key(seed)
        k1, k2, k3 = jax.random.split(key, 3)
        x = jax.random.normal(k1, (B, N, F), dtype=jnp.float32)
        W_qkv = jax.random.normal(k2, (F, F), dtype=jnp.float32) * (1.0 / np.sqrt(F))
        W_o = jax.random.normal(k3, (F, F), dtype=jnp.float32) * (1.0 / np.sqrt(F))
        return {'x': x, 'W_qkv': W_qkv, 'W_o': W_o}
    _L0_attn_in = _L0_attn_setup()

    def _L0_ffn_setup():
        import jax, jax.numpy as jnp
        import numpy as np
        D, H, E, K = (128, 512, 8, 2)
        B, T = (2, 256)

        def _layernorm(x, g, b, eps=1e-05):
            mu = jnp.mean(x, axis=-1, keepdims=True)
            var = jnp.mean(jnp.square(x - mu), axis=-1, keepdims=True)
            return (x - mu) * jax.lax.rsqrt(var + eps) * g + b

        def _expert(x, g, b, W1, b1, W2, b2, Wo, bo):
            x = _layernorm(x, g, b)
            x1 = x @ W1 + b1
            x2 = jnp.clip(x @ W2 + b2, -20.0, 20.0)
            hidden = jnp.clip(x1 * (x2 * jax.nn.sigmoid(x2)), -10000.0, 10000.0)
            return jnp.clip(hidden @ Wo + bo, -10000.0, 10000.0)
        key = jax.random.key(seed)
        ks = jax.random.split(key, 6)
        s = 0.02
        return {'x': jax.random.normal(ks[0], (B, T, D), jnp.float32), 'ln_g': jnp.ones((D,), jnp.float32), 'ln_b': jnp.zeros((D,), jnp.float32), 'router_w': jax.random.normal(ks[1], (D, E), jnp.float32) * s, 'eg': jnp.ones((E, D), jnp.float32), 'eb': jnp.zeros((E, D), jnp.float32), 'W1': jax.random.normal(ks[2], (E, D, H), jnp.float32) * s, 'b1': jnp.zeros((E, H), jnp.float32), 'W2': jax.random.normal(ks[3], (E, D, H), jnp.float32) * s, 'b2': jnp.zeros((E, H), jnp.float32), 'Wo': jax.random.normal(ks[4], (E, H, D), jnp.float32) * s, 'bo': jnp.zeros((E, D), jnp.float32)}
    _L0_ffn_in = _L0_ffn_setup()
    _d = {'L0_attn_x': _L0_attn_in['x'], 'L0_attn_W_qkv': _L0_attn_in['W_qkv'], 'L0_attn_W_o': _L0_attn_in['W_o'], 'L0_ffn_ln_g': _L0_ffn_in['ln_g'], 'L0_ffn_ln_b': _L0_ffn_in['ln_b'], 'L0_ffn_router_w': _L0_ffn_in['router_w'], 'L0_ffn_eg': _L0_ffn_in['eg'], 'L0_ffn_eb': _L0_ffn_in['eb'], 'L0_ffn_W1': _L0_ffn_in['W1'], 'L0_ffn_b1': _L0_ffn_in['b1'], 'L0_ffn_W2': _L0_ffn_in['W2'], 'L0_ffn_b2': _L0_ffn_in['b2'], 'L0_ffn_Wo': _L0_ffn_in['Wo'], 'L0_ffn_bo': _L0_ffn_in['bo']}
    _x0 = _d['L0_attn_x']
    _d['L0_attn_x'] = jax.random.normal(jax.random.fold_in(jax.random.key(seed), 1), (4, 1024, 128), dtype=_x0.dtype)
    del _x0
    return _d

def reference(L0_attn_x, L0_attn_W_qkv, L0_attn_W_o, L0_ffn_ln_g, L0_ffn_ln_b, L0_ffn_router_w, L0_ffn_eg, L0_ffn_eb, L0_ffn_W1, L0_ffn_b1, L0_ffn_W2, L0_ffn_b2, L0_ffn_Wo, L0_ffn_bo):

    def _L0_attn_ref(x, W_qkv, W_o):
        import jax, jax.numpy as jnp
        import numpy as np
        B, N, F, H = (4, 256, 128, 16)
        DH = F // H
        SQRT_D = float(DH) ** 0.5
        b, n, _ = x.shape
        qkv = (x @ W_qkv.T).reshape(b, n, H, DH).transpose(0, 2, 1, 3)
        score = jax.nn.softmax(jnp.einsum('bhif,bhjf->bhij', qkv, qkv) / SQRT_D, axis=-1)
        attn = jnp.einsum('bhij,bhjf->bihf', score, qkv)
        out = attn.reshape(b, n, F) @ W_o.T
        return out

    def _L0_ffn_ref(x, ln_g, ln_b, router_w, eg, eb, W1, b1, W2, b2, Wo, bo):
        import jax, jax.numpy as jnp
        import numpy as np
        D, H, E, K = (128, 512, 8, 2)
        B, T = (2, 256)

        def _layernorm(x, g, b, eps=1e-05):
            mu = jnp.mean(x, axis=-1, keepdims=True)
            var = jnp.mean(jnp.square(x - mu), axis=-1, keepdims=True)
            return (x - mu) * jax.lax.rsqrt(var + eps) * g + b

        def _expert(x, g, b, W1, b1, W2, b2, Wo, bo):
            x = _layernorm(x, g, b)
            x1 = x @ W1 + b1
            x2 = jnp.clip(x @ W2 + b2, -20.0, 20.0)
            hidden = jnp.clip(x1 * (x2 * jax.nn.sigmoid(x2)), -10000.0, 10000.0)
            return jnp.clip(hidden @ Wo + bo, -10000.0, 10000.0)
        Bb, Tt, Dd = x.shape
        xf = _layernorm(x.reshape(-1, Dd), ln_g, ln_b)
        N = xf.shape[0]
        logits = xf @ router_w
        scores, idx = jax.lax.top_k(logits, K)
        gate = jax.nn.softmax(scores, axis=-1)
        gates_e = jnp.zeros((N, E), xf.dtype).at[jnp.arange(N)[:, None], idx].add(gate)

        def body(acc, p):
            gcol, g, b, w1, bb1, w2, bb2, wo, bbo = p
            return (acc + gcol[:, None] * _expert(xf, g, b, w1, bb1, w2, bb2, wo, bbo), None)
        out, _ = jax.lax.scan(body, jnp.zeros_like(xf), (gates_e.T, eg, eb, W1, b1, W2, b2, Wo, bo))
        return out.reshape(Bb, Tt, Dd)
    x = L0_attn_x
    x = x + 0.5 * _L0_ffn_ref(_layernorm(x, axis=-1), L0_ffn_ln_g, L0_ffn_ln_b, L0_ffn_router_w, L0_ffn_eg, L0_ffn_eb, L0_ffn_W1, L0_ffn_b1, L0_ffn_W2, L0_ffn_b2, L0_ffn_Wo, L0_ffn_bo)
    x = x + _L0_attn_ref(_layernorm(x, axis=-1), L0_attn_W_qkv, L0_attn_W_o)
    x = x + 0.5 * _L0_ffn_ref(_layernorm(x, axis=-1), L0_ffn_ln_g, L0_ffn_ln_b, L0_ffn_router_w, L0_ffn_eg, L0_ffn_eb, L0_ffn_W1, L0_ffn_b1, L0_ffn_W2, L0_ffn_b2, L0_ffn_Wo, L0_ffn_bo)
    return x

_drawn_inputs = setup_inputs


def setup_inputs(seed=0):
    import zlib

    import numpy as np

    out = dict(_drawn_inputs(seed))
    spreads = {'L0_ffn_ln_g': (1.0, 0.6),
     'L0_ffn_ln_b': (0.0, 0.441),
     'L0_ffn_eg': (1.0, 0.6),
     'L0_ffn_eb': (0.0, 0.8),
     'L0_ffn_b1': (0.0, 0.8),
     'L0_ffn_b2': (0.0, 0.8),
     'L0_ffn_bo': (0.0, 0.1)}
    factors = {'L0_ffn_W1': 6.827, 'L0_ffn_W2': 6.864, 'L0_ffn_Wo': 6.298}
    for name, (base, spread) in spreads.items():
        noise = np.random.default_rng([zlib.crc32(name.encode()), seed]).standard_normal(out[name].shape)
        drawn = base * np.exp(spread * noise) if base else spread * noise
        out[name] = jnp.asarray(drawn.astype(out[name].dtype))
    for name, factor in factors.items():
        out[name] = (out[name] * factor).astype(out[name].dtype)
    return out
```

```python
import concourse.bass as bass
from concourse import mybir
from contextlib import ExitStack
from collections import deque

F32 = mybir.dt.float32
BF16 = mybir.dt.bfloat16
ALU = mybir.AluOpType
ACT = mybir.ActivationFunctionType
AX = mybir.AxisListType


class Token:

    def __init__(self, sem, value):
        self.sem, self.value = sem, value


class Queue:

    def __init__(self, engine, sem):
        self.engine, self.sem, self.count, self.items, self.seen = engine, sem, 0, [], {}

    def wait(self, *tokens):
        for token in tokens:
            if token is not None and self.seen.get(id(token.sem), 0) < token.value:
                self.seen[id(token.sem)] = token.value
                self.items.append((self.engine.wait_ge, (token.sem, token.value), {}, None))

    def do(self, op, /, *args, **kwargs):
        self.items.append((op, args, kwargs, None))

    def mark(self, op, /, *args, **kwargs):
        self.count += 1
        self.items.append((op, args, kwargs, (self.sem, 1)))
        return Token(self.sem, self.count)

    def then(self, op, /, *args, **kwargs):
        token = self.mark(op, *args, **kwargs)
        self.wait(token)
        return token

    def dma(self, lane, out, in_):
        lane.count += 16
        self.items.append((self.engine.dma_start, (out, in_), {}, (lane.sem, 16)))
        return Token(lane.sem, lane.count)

    def play(self):
        for op, args, kwargs, inc in self.items:
            instruction = op(*args, **kwargs)
            if inc:
                instruction.then_inc(*inc)


class Lane:

    def __init__(self, sem):
        self.sem, self.count = sem, 0


def build_macaron(nc, x, w_qkv, w_o, ln_g, ln_b, router_w, eg, eb, w1, b1, w2, b2, wo, bo, out):
    P = 128
    B, N, F = x.shape
    E, D, H = w1.shape
    HEADS = 16
    DH = F // HEADS
    SCALE = 1.0 / float(DH) ** 0.5
    EPS = 1e-5
    HC = H // P
    BT = N // P
    T = B * BT
    GT = 4
    GW = GT * P
    NG = T // GT
    X2_LIMIT, LIMIT = 20.0, 10000.0

    stack = ExitStack()
    with stack:
        def sbuf(name, shape, dt=F32, owner=stack):
            return owner.enter_context(nc.sbuf_tensor(name, shape, dt))

        def semaphore(name):
            return stack.enter_context(nc.semaphore(name))

        pe = Queue(nc.tensor, semaphore("pe_done"))
        act = Queue(nc.scalar, semaphore("act_done"))
        dve = Queue(nc.vector, semaphore("dve_done"))
        pool = Queue(nc.gpsimd, semaphore("pool_done"))
        sp = Queue(nc.sync, semaphore("sp_done"))
        V, G, S, TE = nc.vector, nc.gpsimd, nc.scalar, nc.tensor

        x_sb = sbuf("x_sb", [P, T, F])
        w1_sb = sbuf("w1_sb", [P, E, H])
        w2_sb = sbuf("w2_sb", [P, E, H])
        wo_sb = sbuf("wo_sb", [P, E, HC, F])
        bo_bc = sbuf("bo_bc", [P, E, F])
        ln_g_bc = sbuf("ln_g_bc", [P, F])
        ln_b_bc = sbuf("ln_b_bc", [P, F])
        router_sb = sbuf("router_sb", [P, E])
        identity = sbuf("identity", [P, P])
        earlier = sbuf("earlier", [P, E, E])
        minus_half = sbuf("minus_half", [P, 1])
        VEC = 2 * E + 2 * E * HC
        vec_rows = sbuf("vec_rows", [VEC, P])
        vecs = sbuf("vecs", [P, VEC])
        eg_col, eb_col = vecs[:, 0:E], vecs[:, E:2 * E]
        b_col = [vecs[:, 2 * E:2 * E + E * HC], vecs[:, 2 * E + E * HC:VEC]]
        bias1 = sbuf("bias1", [P, E * HC])
        bias2 = sbuf("bias2", [P, E * HC])
        clip_lo = sbuf("clip_lo", [P, E * HC])
        clip_hi = sbuf("clip_hi", [P, E * HC])
        wqkv_t = sbuf("wqkv_t", [P, P])
        wo_t = sbuf("wo_t", [P, P])

        bank = [stack.enter_context(nc.psum_tensor(f"bank{i}", [P, 512], F32)) for i in range(4)]
        wide = [stack.enter_context(nc.psum_tensor(f"wide{i}", [P, 1024], F32)) for i in range(2)]

        lane_x = [Lane(semaphore(f"x_in{b}")) for b in range(B)]
        lane_const = Lane(semaphore("const_in"))
        lane_w = [Lane(semaphore(f"expert_in{e}")) for e in range(E)]
        lane_out = Lane(semaphore("x_out"))

        x_in = []

        def load_x(b):
            x_in.append(sp.dma(lane_x[b], x_sb[:, b * BT:(b + 1) * BT, :],
                               x[b].rearrange("(p t) f -> p t f", p=P)))

        load_x(0)
        sp.dma(lane_const, vec_rows[0:E, :], eg)
        sp.dma(lane_const, vec_rows[E:2 * E, :], eb)
        sp.dma(lane_const, vec_rows[2 * E:2 * E + E * HC, :], b1.rearrange("e (c p) -> (e c) p", p=P))
        sp.dma(lane_const, vec_rows[2 * E + E * HC:VEC, :], b2.rearrange("e (c p) -> (e c) p", p=P))
        sp.dma(lane_const, ln_g_bc[:, :], ln_g.unsqueeze(0).to_broadcast([P, F]))
        sp.dma(lane_const, ln_b_bc[:, :], ln_b.unsqueeze(0).to_broadcast([P, F]))
        sp.dma(lane_const, router_sb[:, :], router_w)
        const_in = sp.dma(lane_const, bo_bc[:, :, :], bo.unsqueeze(0).to_broadcast([P, E, F]))
        expert_in = []
        for e in range(E):
            sp.dma(lane_w[e], w1_sb[:, e, :], w1[e])
            sp.dma(lane_w[e], w2_sb[:, e, :], w2[e])
            expert_in.append(sp.dma(lane_w[e], wo_sb[:, e, :, :],
                                    wo[e].rearrange("(c p) d -> p c d", p=P)))
            if e == 0:
                for b in range(1, B):
                    load_x(b)

        pool.then(G.memset, identity[:, :], 0.0)
        identity_made = pool.then(G.affine_select, out=identity[:, :], in_=identity[:, :],
                                  compare_op=ALU.not_equal, fill=1.0, base=0,
                                  pattern=[[-1, P]], channel_multiplier=1)
        pool.do(G.memset, minus_half[:, :], -0.5)
        pool.then(G.memset, earlier[:, :, :], 1.0)
        earlier_made = pool.then(G.affine_select, out=earlier[:, :, :], in_=earlier[:, :, :],
                                 compare_op=ALU.is_gt, fill=0.0, base=0,
                                 pattern=[[1, E], [-1, E]], channel_multiplier=0)

        def row_statistics(src, ntiles, stats, mean_var, shifted):
            for t in range(ntiles):
                last = dve.mark(V.bn_stats, out=stats[:, t, :], in_=src[:, t, :])
            dve.wait(last)
            for t in range(ntiles):
                last = dve.mark(V.bn_aggr, out=mean_var[:, t, :], in_=stats[:, t, :])
            dve.wait(last)
            return dve.mark(V.tensor_scalar_add, shifted[:, 0:ntiles], mean_var[:, 0:ntiles, 1], EPS)

        def inverse_deviation(ready, rstd, shifted, ntiles):
            pool.wait(ready)
            return pool.mark(G.tensor_tensor, rstd[:, 0:ntiles], shifted[:, 0:ntiles],
                             minus_half[:, 0:1].to_broadcast([P, ntiles]), ALU.pow)

        def normalise(ready, dst, src, ntiles, mean_var, rstd):
            dve.wait(ready)
            for t in range(ntiles):
                last = dve.mark(V.tensor_scalar, dst[:, t, :], src[:, t, :], mean_var[:, t, 0:1],
                                rstd[:, t:t + 1], ALU.subtract, ALU.mult)
            return last

        def fold_expert_vectors():
            pe.wait(const_in, identity_made)
            turned = pe.mark(TE.transpose, bank[0][:, 0:VEC], vec_rows[:, :], identity[0:VEC, 0:VEC])
            dve.wait(turned)
            copied = dve.then(V.tensor_copy, vecs[:, :], bank[0][:, 0:VEC])
            pe.wait(copied)
            for e in range(E):
                pe.wait(expert_in[e])
                for k, w in enumerate((w1_sb, w2_sb)):
                    for c in range(HC):
                        last = pe.mark(TE.matmul, bank[1 + k][:, e * HC + c:e * HC + c + 1],
                                       w[:, e, c * P:(c + 1) * P], eb_col[:, e:e + 1],
                                       start=True, stop=True)
                dve.wait(last)
                for w in (w1_sb, w2_sb):
                    scaled = dve.mark(V.tensor_scalar, w[:, e, :], w[:, e, :], eg_col[:, e:e + 1],
                                      None, ALU.mult)
            dve.do(V.tensor_tensor, bias1[:, :], bank[1][:, 0:E * HC], b_col[0], ALU.add)
            dve.then(V.tensor_tensor, bias2[:, :], bank[2][:, 0:E * HC], b_col[1], ALU.add)
            dve.do(V.tensor_scalar, clip_lo[:, :], bias2[:, :], -1.0, -X2_LIMIT, ALU.mult, ALU.add)
            return dve.then(V.tensor_scalar, clip_hi[:, :], bias2[:, :], -1.0, X2_LIMIT, ALU.mult, ALU.add)

        def ffn(tag, start, folded=None, store=False):
            own = ExitStack()

            def buf(name, shape, dt=F32):
                return sbuf(f"{tag}_{name}", shape, dt, own)

            normed = buf("normed", [P, GT, F])
            xf = buf("xf", [P, GT, F])
            xe = buf("xe", [P, GT, F])
            stats = buf("stats", [P, GT, 6])
            mean_var = buf("mean_var", [P, GT, 2])
            shifted = buf("shifted", [P, GT])
            rstd = buf("rstd", [P, GT])
            xf_t = buf("xf_t", [P, GW])
            xe_t = buf("xe_t", [P, 2, GW])
            logits = buf("logits", [P, GT, E])
            above = buf("above", [P, GT, E, E])
            at_least = buf("at_least", [P, GT, E, E])
            rank = buf("rank", [P, GT, E])
            is_top = [buf(f"is_top{k}", [P, GT, E]) for k in range(2)]
            top = [buf(f"top{k}", [P, GT]) for k in range(2)]
            lead = buf("lead", [P, GT])
            share = [buf(f"share{k}", [P, GT]) for k in range(2)]
            gates = buf("gates", [P, 2, GT, E])
            x2c = buf("x2c", [P, 2, GW])
            silu = buf("silu", [P, 2, GW])
            hidden = buf("hidden", [P, 2, HC, GW])
            y = buf("y", [P, GT, F])
            acc = buf("acc", [P, GT, F])

            pair = [(wide[i][:, 0:GW], wide[i][:, GW:2 * GW]) for i in range(2)]
            y_bank = bank[0:2]
            turn_bank = bank[2:4]
            turn_free = [None, None]
            xe_t_free = [None, None]
            gates_of, xe_t_of = {}, {}

            for q in (dve, act, pool, pe):
                q.wait(*start)

            def prologue(g):
                src = x_sb[:, g * GT:(g + 1) * GT, :]
                if tag == "ffn1":
                    dve.wait(x_in[g * GT // BT])
                ready = inverse_deviation(row_statistics(src, GT, stats, mean_var, shifted),
                                          rstd, shifted, GT)
                yield
                dve.wait(normalise(ready, normed, src, GT, mean_var, rstd))
                ready = inverse_deviation(row_statistics(normed, GT, stats, mean_var, shifted),
                                          rstd, shifted, GT)
                yield
                dve.wait(turn_free[0])
                dve.wait(normalise(ready, xf, normed, GT, mean_var, rstd))
                dve.wait(const_in)
                dve.then(V.tensor_tensor, xf[:, :, :], xf[:, :, :],
                         ln_g_bc[:, :].unsqueeze(1).to_broadcast([P, GT, F]), ALU.mult)
                xf_ready = dve.then(V.tensor_tensor, xf[:, :, :], xf[:, :, :],
                                    ln_b_bc[:, :].unsqueeze(1).to_broadcast([P, GT, F]), ALU.add)
                ready = inverse_deviation(row_statistics(xf, GT, stats, mean_var, shifted),
                                          rstd, shifted, GT)
                yield
                dve.wait(turn_free[1])
                xe_ready = normalise(ready, xe, xf, GT, mean_var, rstd)
                yield
                pe.wait(xf_ready, identity_made, turn_free[0])
                for t in range(GT):
                    last = pe.mark(TE.transpose, turn_bank[0][:, t * P:(t + 1) * P], xf[:, t, :],
                                   identity[:, :])
                act.wait(last)
                xf_t_ready = act.mark(S.copy, xf_t[:, :], turn_bank[0][:, :])
                pe.wait(xe_ready, turn_free[1])
                for t in range(GT):
                    last = pe.mark(TE.transpose, turn_bank[1][:, t * P:(t + 1) * P], xe[:, t, :],
                                   identity[:, :])
                act.wait(last, xe_t_free[g % 2])
                xe_t_of[g] = turn_free[1] = act.mark(S.copy, xe_t[:, g % 2, :], turn_bank[1][:, :])
                yield
                pe.wait(xf_t_ready)
                for t in range(GT):
                    last = pe.mark(TE.matmul, turn_bank[0][:, t * E:(t + 1) * E],
                                   xf_t[:, t * P:(t + 1) * P], router_sb[:, :], start=True, stop=True)
                dve.wait(last)
                turn_free[0] = dve.then(V.tensor_copy, logits[:, :, :],
                                        turn_bank[0][:, 0:GT * E].rearrange("p (t e) -> p t e", e=E))
                other = logits[:, :, :].unsqueeze(2).to_broadcast([P, GT, E, E])
                mine = logits[:, :, :].unsqueeze(3).to_broadcast([P, GT, E, E])
                dve.do(V.tensor_tensor, above[:, :, :, :], other, mine, ALU.is_gt)
                dve.then(V.tensor_tensor, at_least[:, :, :, :], other, mine, ALU.is_ge)
                dve.then(V.tensor_tensor, at_least[:, :, :, :], at_least[:, :, :, :], above[:, :, :, :],
                         ALU.subtract)
                dve.wait(earlier_made)
                dve.then(V.tensor_tensor, at_least[:, :, :, :], at_least[:, :, :, :],
                         earlier[:, :, :].unsqueeze(1).to_broadcast([P, GT, E, E]), ALU.mult)
                dve.then(V.tensor_tensor, above[:, :, :, :], above[:, :, :, :], at_least[:, :, :, :], ALU.add)
                dve.then(V.tensor_reduce, out=rank[:, :, :], in_=above[:, :, :, :], axis=AX.X, op=ALU.add)
                yield
                for k in range(2):
                    dve.then(V.tensor_scalar, is_top[k][:, :, :], rank[:, :, :], float(k), None, ALU.is_equal)
                    dve.then(V.tensor_tensor, above[:, :, 0, :], logits[:, :, :], is_top[k][:, :, :], ALU.mult)
                    dve.then(V.tensor_reduce, out=top[k][:, :], in_=above[:, :, 0, :], axis=AX.X, op=ALU.add)
                led = dve.mark(V.tensor_tensor, lead[:, :], top[0][:, :], top[1][:, :], ALU.subtract)
                act.wait(led)
                act.do(S.activation, share[0][:, :], lead[:, :], ACT.Sigmoid)
                shared = act.mark(S.activation, share[1][:, :], lead[:, :], ACT.Sigmoid, scale=-1.0)
                yield
                dve.wait(shared)
                for k in range(2):
                    dve.then(V.tensor_tensor, is_top[k][:, :, :], is_top[k][:, :, :],
                             share[k][:, :].unsqueeze(2).to_broadcast([P, GT, E]), ALU.mult)
                gates_of[g] = dve.then(V.tensor_tensor, gates[:, g % 2, :, :], is_top[0][:, :, :],
                                       is_top[1][:, :, :], ALU.add)

            for _ in prologue(0):
                pass
            if folded is None:
                folded = fold_expert_vectors()
            dve_silu_in, act_silu_out, hidden_ready = {}, {}, {}
            x1_free = [None, None]
            hidden_free = [None, None]
            y_free = [None, None]
            order = [(g, e) for g in range(NG) for e in range(E)]
            count = 0
            waiting = None
            ended = []

            def combine(item):
                k, c, n, silu_ready = item
                g, e = order[k]
                j = e * HC + c
                dve.wait(silu_ready, hidden_free[k % 2])
                made = x1_free[n % 2] = dve.mark(
                    V.scalar_tensor_tensor, hidden[:, k % 2, c, :], pair[n % 2][0], bias1[:, j:j + 1],
                    silu[:, n % 2, :], ALU.add, ALU.mult)
                pool.wait(made)
                hidden_ready[k, c] = pool.mark(G.tensor_scalar, hidden[:, k % 2, c, :],
                                               hidden[:, k % 2, c, :], LIMIT, -LIMIT, ALU.min, ALU.max)

            def second_product(k):
                g, e = order[k]
                pe.wait(y_free[k % 2], *[hidden_ready[k, c] for c in range(HC)])
                for t in range(GT):
                    for c in range(HC):
                        last = (pe.mark if (t, c) == (GT - 1, HC - 1) else pe.do)(
                            TE.matmul, y_bank[k % 2][:, t * P:(t + 1) * P],
                            hidden[:, k % 2, c, t * P:(t + 1) * P], wo_sb[:, e, c, :],
                            start=(c == 0), stop=(c == HC - 1))
                hidden_free[k % 2] = last
                return last

            def add_expert(k, product):
                g, e = order[k]
                dve.wait(product)
                y_free[k % 2] = dve.then(
                    V.tensor_tensor, y[:, :, :], y_bank[k % 2][:, :].rearrange("p (t f) -> p t f", f=F),
                    bo_bc[:, e, :].unsqueeze(1).to_broadcast([P, GT, F]), ALU.add)
                dve.then(V.tensor_scalar, y[:, :, :], y[:, :, :], LIMIT, -LIMIT, ALU.min, ALU.max)
                gate = gates[:, g % 2, :, e].unsqueeze(2).to_broadcast([P, GT, F])
                if e == 0:
                    dve.then(V.tensor_tensor, acc[:, :, :], y[:, :, :], gate, ALU.mult)
                else:
                    dve.then(V.tensor_tensor, y[:, :, :], y[:, :, :], gate, ALU.mult)
                    dve.then(V.tensor_tensor, acc[:, :, :], acc[:, :, :], y[:, :, :], ALU.add)
                if e == E - 1:
                    rows = x_sb[:, g * GT:(g + 1) * GT, :]
                    done = dve.then(V.scalar_tensor_tensor, rows, acc[:, :, :], 0.5, rows, ALU.mult, ALU.add)
                    if store:
                        sp.wait(done)
                        b, t0 = divmod(g * GT, BT)
                        ended[:] = [sp.dma(lane_out, out[b].rearrange("(p t) f -> p t f", p=P)
                                           [:, t0:t0 + GT, :], rows)]
                    else:
                        ended[:] = [done]

            side = iter(())
            product = None
            for k, (g, e) in enumerate(order):
                if e == 0:
                    for _ in side:
                        pass
                    side = prologue(g + 1) if g + 1 < NG else iter(())
                if k == 0:
                    pe.wait(folded)
                pe.wait(xe_t_of[g])
                dve.wait(gates_of[g])
                for c in range(HC):
                    j = e * HC + c
                    pe.wait(x1_free[count % 2])
                    pe.do(TE.matmul, pair[count % 2][1], w2_sb[:, e, c * P:(c + 1) * P], xe_t[:, g % 2, :],
                          start=True, stop=True)
                    first = pe.mark(TE.matmul, pair[count % 2][0], w1_sb[:, e, c * P:(c + 1) * P],
                                    xe_t[:, g % 2, :], start=True, stop=True)
                    dve.wait(first, act_silu_out.get(count - 2))
                    clipped = dve.mark(V.tensor_scalar, x2c[:, count % 2, :], pair[count % 2][1],
                                       clip_lo[:, j:j + 1], clip_hi[:, j:j + 1], ALU.max, ALU.min)
                    act.wait(clipped, x1_free[count % 2])
                    act_silu_out[count] = act.mark(S.activation, silu[:, count % 2, :], x2c[:, count % 2, :],
                                                   ACT.Silu, bias=bias2[:, j:j + 1])
                    if waiting:
                        combine(waiting)
                    waiting = (k, c, count, act_silu_out[count])
                    count += 1
                    if c == 1 and k:
                        product = second_product(k - 1)
                    if c == 2 and k:
                        add_expert(k - 1, product)
                xe_t_free[g % 2] = first
                next(side, None)
            combine(waiting)
            add_expert(len(order) - 1, second_product(len(order) - 1))
            own.close()
            return ended + [hidden_free[0], hidden_free[1]]

        def attention(start):
            own = ExitStack()

            def buf(name, shape, dt=F32):
                return sbuf(f"att_{name}", shape, dt, own)

            PARTS = 3
            ROWS = DH * PARTS * PARTS
            KROWS = ROWS + PARTS
            TEAM = 4
            TEAMS = HEADS // TEAM
            HALF = N // 2
            HT = HALF // P
            SLOTS = 3
            VW = P // TEAM
            NTEAM = B * TEAMS

            xh = buf("xh", [P, BT, F])
            stats = buf("stats", [P, BT, 6])
            mean_var = buf("mean_var", [P, BT, 2])
            shifted = buf("shifted", [P, BT])
            rstd = buf("rstd", [P, BT])
            q_t = buf("q_t", [P, N])
            rest = xh[:, :, :].rearrange("p t f -> p (t f)")
            attn_t = xh_t = buf("xh_t", [P, N])
            parts = buf("parts", [P, PARTS, N], BF16)
            left = buf("left", [P, SLOTS, TEAM, N], BF16)
            right = buf("right", [P, SLOTS, TEAM, N], BF16)
            values = buf("values", [P, 2, BT, HEADS, VW])
            neg_max = buf("neg_max", [P, 2, TEAM, BT])
            max_rest = buf("max_rest", [TEAM * BT, P])
            max_parts = buf("max_parts", [TEAM * BT, 2, PARTS, P], BF16)
            PROBS = 2 * TEAM
            probs = buf("probs", [P, PROBS, HALF])
            o_t = buf("o_t", [P, 2, HALF])
            inv_sum = buf("inv_sum", [P, HT, TEAM])
            attn = buf("attn", [P, BT, F])
            q_dram = nc.dram_tensor("q_parts_dram", [B, P, PARTS, N], BF16)

            max_dram = nc.dram_tensor("max_parts_dram", [NTEAM, TEAM * BT, PARTS, P], BF16)

            lane_max_out = Lane(semaphore("max_parts_out"))
            lane_q = Lane(semaphore("q_parts_out"))
            lane_lr = [Lane(semaphore(f"operands_in{s}")) for s in range(SLOTS)]
            lane_max = [Lane(semaphore(f"max_in{s}")) for s in range(SLOTS)]
            score_bank = bank[0:3]
            value_bank = bank[3]

            for queue in (dve, act, pool, pe, sp):
                queue.wait(*start)

            wide_free, taken = [None, None], [0]

            def take_wide():
                n = taken[0] % 2
                taken[0] += 1
                pe.wait(wide_free[n])
                return n

            w_rows = [o_t[:, 0, 0:P], o_t[:, 0, P:2 * P]]
            lane_wa = Lane(semaphore("attention_weights_in"))
            sp.dma(lane_wa, w_rows[0], w_qkv)
            weights_in = sp.dma(lane_wa, w_rows[1], w_o)
            n = take_wide()
            pe.wait(weights_in)
            pe.do(TE.transpose, wide[n][:, 0:P], w_rows[0], identity[:, :])
            last = pe.mark(TE.transpose, wide[n][:, P:2 * P], w_rows[1], identity[:, :])
            act.wait(last)
            act.do(S.copy, wqkv_t[:, :], wide[n][:, 0:P])
            weights_turned = wide_free[n] = act.mark(S.copy, wo_t[:, :], wide[n][:, P:2 * P])

            ones = pool.mark(G.memset, left[:, :, :, :], 1.0)
            pool.then(G.memset, values[:, :, :, :, :], 0.0)
            values_blank = pool.mark(G.memset, values[:, :, :, :, DH:DH + 1], 1.0)

            q_out, values_ready, values_free = {}, {}, {}

            def prepare(b):
                src = x_sb[:, b * BT:(b + 1) * BT, :]
                ready = inverse_deviation(row_statistics(src, BT, stats, mean_var, shifted),
                                          rstd, shifted, BT)
                yield
                normed = normalise(ready, xh, src, BT, mean_var, rstd)
                yield
                n = take_wide()
                pe.wait(normed)
                for t in range(BT):
                    last = pe.mark(TE.transpose, wide[n][:, t * P:(t + 1) * P], xh[:, t, :], identity[:, :])
                act.wait(last)
                turned = wide_free[n] = act.mark(S.copy, xh_t[:, :], wide[n][:, :])
                yield
                n = take_wide()
                pe.wait(turned, weights_turned)
                for h in range(2):
                    last = pe.mark(TE.matmul, wide[n][:, h * HALF:(h + 1) * HALF], wqkv_t[:, :],
                                   xh_t[:, h * HALF:(h + 1) * HALF], start=True, stop=True)
                act.wait(last)
                projected = wide_free[n] = act.mark(S.copy, q_t[:, :], wide[n][:, :])
                yield
                dve.wait(projected, q_out.get(b - 1))
                dve.then(V.tensor_copy, parts[:, 0, :], q_t[:, :])
                dve.then(V.tensor_tensor, rest, q_t[:, :], parts[:, 0, :], ALU.subtract)
                dve.then(V.tensor_copy, parts[:, 1, :], rest)
                dve.then(V.tensor_tensor, rest, rest, parts[:, 1, :], ALU.subtract)
                split = dve.then(V.tensor_copy, parts[:, 2, :], rest)
                sp.wait(split)
                q_out[b] = sp.dma(lane_q, q_dram[b], parts[:, :, :])
                yield
                n = take_wide()
                pe.wait(projected)
                for t in range(BT):
                    last = pe.mark(TE.transpose, wide[n][:, t * P:(t + 1) * P], q_t[:, t * P:(t + 1) * P],
                                   identity[:, :])
                act.wait(last, values_free.get(b - 2), values_blank)
                values_ready[b] = wide_free[n] = act.mark(
                    S.copy, values[:, b % 2, :, :, 0:DH].rearrange("p t h d -> p (t h) d"),
                    wide[n][:, :].rearrange("p (th d) -> p th d", d=DH))

            operands_in, scores_done = {}, {}

            def load_operands(i):
                b, team = divmod(i, TEAMS)
                s = i % SLOTS
                sp.wait(q_out[b], ones, scores_done.get(i - SLOTS))
                heads = q_dram[b, team * TEAM * DH:(team + 1) * TEAM * DH, :, :]
                for k in range(PARTS):
                    block = slice(k * DH * PARTS, (k + 1) * DH * PARTS)
                    sp.dma(lane_lr[s], left[block, s, :, :],
                           heads.rearrange("(h d) j n -> (d j) h n", d=DH))
                    for j in range(TEAM):
                        operands_in[i] = sp.dma(
                            lane_lr[s], right[block, s, j, :],
                            heads[j * DH:(j + 1) * DH, k:k + 1, :].to_broadcast([DH, PARTS, N]))

            def row_max(i, j, t):
                n = take_wide()
                s = i % SLOTS
                pe.wait(operands_in[i])
                for h in range(2):
                    last = (pe.do, pe.mark)[h](
                        TE.matmul, wide[n][:, h * HALF:(h + 1) * HALF], left[0:ROWS, s, j, t * P:(t + 1) * P],
                        right[0:ROWS, s, j, h * HALF:(h + 1) * HALF], start=True, stop=True)
                dve.wait(last)
                wide_free[n] = dve.mark(V.tensor_reduce, out=neg_max[:, i % 2, j, t:t + 1], in_=wide[n][:, :],
                                        axis=AX.X, op=ALU.max, negate=True)
                return wide_free[n]

            max_in, max_out = {}, {}

            def place_max(i, reduced):
                n = take_wide()
                s = i % SLOTS
                pe.wait(reduced)
                turned = pe.mark(TE.transpose, wide[n][0:TEAM * BT, 0:P],
                                 neg_max[:, i % 2, :, :].rearrange("p j t -> p (j t)"), identity[:, :])
                mine = max_parts[:, i % 2, :, :]
                dve.wait(turned, max_out.get(i - 2))
                wide_free[n] = dve.then(V.tensor_copy, max_rest[:, :], wide[n][0:TEAM * BT, 0:P])
                for k in range(PARTS):
                    last = dve.then(V.tensor_copy, mine[:, k, :], max_rest[:, :])
                    if k < PARTS - 1:
                        dve.then(V.tensor_tensor, max_rest[:, :], max_rest[:, :], mine[:, k, :], ALU.subtract)
                sp.wait(last)
                max_out[i] = sp.dma(lane_max_out, max_dram[i], mine)
                sp.wait(max_out[i])
                for j in range(TEAM):
                    max_in[i] = sp.dma(lane_max[s], right[ROWS:KROWS, s, j, :].rearrange("k (t q) -> k t q", q=P),
                                       max_dram[i, j * BT:(j + 1) * BT, :, :].rearrange("t k q -> k t q"))

            attn_free = [None]
            o_free = [None, None]
            value_free = [None]
            ended = []

            def finish_half(i, half, summed):
                b, team = divmod(i, TEAMS)
                act.wait(summed, o_free[half])
                copied = value_free[0] = act.mark(S.copy, o_t[:, half, :], value_bank[:, :])
                yield
                n = take_wide()
                pe.wait(copied)
                for t in range(HT):
                    last = pe.mark(TE.transpose, wide[n][:, t * P:(t + 1) * P],
                                   o_t[:, half, t * P:(t + 1) * P], identity[:, :])
                o_free[half] = last
                o = wide[n][:, 0:HT * P].rearrange("p (t j d) -> p t j d", t=HT, j=TEAM)
                dve.wait(last, attn_free[0])
                dve.then(V.reciprocal, inv_sum[:, :, :], o[:, :, :, DH])
                where = attn[:, half * HT:(half + 1) * HT, team * TEAM * DH:(team + 1) * TEAM * DH]
                placed = wide_free[n] = dve.then(
                    V.tensor_tensor, where.rearrange("p t (j d) -> p t j d", j=TEAM), o[:, :, :, 0:DH],
                    inv_sum[:, :, :].unsqueeze(3).to_broadcast([P, HT, TEAM, DH]), ALU.mult)
                yield
                if (team, half) != (TEAMS - 1, 1):
                    return
                n = take_wide()
                pe.wait(placed)
                for t in range(BT):
                    last = pe.mark(TE.transpose, wide[n][:, t * P:(t + 1) * P], attn[:, t, :], identity[:, :])
                attn_free[0] = last
                act.wait(last)
                turned = wide_free[n] = act.mark(S.copy, attn_t[:, :], wide[n][:, :])
                yield
                n = take_wide()
                pe.wait(turned)
                for t in range(BT):
                    last = pe.mark(TE.matmul, wide[n][:, t * P:(t + 1) * P], attn_t[:, t * P:(t + 1) * P],
                                   wo_t[:, :], start=True, stop=True)
                rows = x_sb[:, b * BT:(b + 1) * BT, :]
                dve.wait(last)
                wide_free[n] = dve.then(V.tensor_tensor, rows, rows,
                                        wide[n][:, :].rearrange("p (t f) -> p t f", f=F), ALU.add)
                ended[:] = [wide_free[n], last]

            for _ in prepare(0):
                pass
            load_operands(0)
            load_operands(1)
            for j in range(TEAM):
                for t in range(BT):
                    reduced = row_max(0, j, t)
            place_max(0, reduced)

            UNITS = 2 * BT
            MAXIMA = [3 if u % 2 == 0 and u < 12 else 2 for u in range(UNITS - 3)] + [0, 0, 0]
            assert sum(MAXIMA) == TEAM * BT
            jobs = deque()
            score_free = [None] * 3
            probs_free = [None] * PROBS
            exp_of = {}
            scored = 0
            previous = None

            def value_product(unit):
                i, half, kt, first = unit
                b, team = divmod(i, TEAMS)
                pe.wait(values_ready[b])
                if kt == 0:
                    pe.wait(value_free[0])
                for j in range(TEAM):
                    pe.wait(exp_of[first + j])
                    last = (pe.mark if j == TEAM - 1 else pe.do)(
                        TE.matmul, value_bank[j * VW:(j + 1) * VW, :], values[:, b % 2, kt, team * TEAM + j, :],
                        probs[:, (first + j) % PROBS, :], start=(kt == 0), stop=(kt == BT - 1))
                for j in range(TEAM):
                    probs_free[(first + j) % PROBS] = last
                values_free[b] = last
                if kt == BT - 1:
                    jobs.append(finish_half(i, half, last))
                    next(jobs[-1])

            def next_job():
                while jobs:
                    try:
                        next(jobs[0])
                        return
                    except StopIteration:
                        jobs.popleft()

            for i in range(NTEAM):
                b, team = divmod(i, TEAMS)
                s = i % SLOTS
                if i + 2 < NTEAM:
                    if (i + 2) % TEAMS == 0:
                        while (i + 2) // TEAMS not in values_ready:
                            next_job()
                    load_operands(i + 2)
                if team == 1 and b + 1 < B:
                    jobs.append(prepare(b + 1))
                pairs = iter([(j, t) for j in range(TEAM) for t in range(BT)]) if i + 1 < NTEAM else iter(())
                pe.wait(max_in[i])
                for u in range(UNITS):
                    half, kt = divmod(u, BT)
                    first = scored
                    maxima = MAXIMA[u]
                    for j in range(TEAM):
                        n = scored % 3
                        pe.wait(score_free[n])
                        scores = pe.mark(TE.matmul, score_bank[n][:, :], left[0:KROWS, s, j, kt * P:(kt + 1) * P],
                                         right[0:KROWS, s, j, half * HALF:(half + 1) * HALF],
                                         start=True, stop=True)
                        act.wait(scores, probs_free[scored % PROBS])
                        exp_of[scored] = score_free[n] = act.mark(
                            S.activation, probs[:, scored % PROBS, :], score_bank[n][:, :], ACT.Exp, scale=SCALE)
                        scored += 1
                        if j and maxima:
                            pair = next(pairs, None)
                            if pair:
                                reduced = row_max(i + 1, *pair)
                            maxima -= 1
                    if previous:
                        value_product(previous)
                    previous = (i, half, kt, first)
                    if i + 1 < NTEAM and u == UNITS - 3:
                        place_max(i + 1, reduced)
                    next_job()
                scores_done[i] = scores
            value_product(previous)
            while jobs:
                next_job()
            own.close()
            return ended

        start = ffn("ffn1", [])
        start = attention(start)
        ended = ffn("ffn2", start, folded=start[0], store=True)
        sp.wait(*ended)

        block = stack.enter_context(nc.Block())

        @block.sync
        def _(engine):
            sp.play()

        @block.gpsimd
        def _(engine):
            pool.play()

        @block.scalar
        def _(engine):
            act.play()

        @block.vector
        def _(engine):
            dve.play()

        @block.tensor
        def _(engine):
            pe.play()


_INS = ["L0_attn_x", "L0_attn_W_qkv", "L0_attn_W_o", "L0_ffn_ln_g", "L0_ffn_ln_b", "L0_ffn_router_w",
        "L0_ffn_eg", "L0_ffn_eb", "L0_ffn_W1", "L0_ffn_b1", "L0_ffn_W2", "L0_ffn_b2", "L0_ffn_Wo", "L0_ffn_bo"]


def kernel(**inputs):
    import numpy as _np
    import concourse.bacc as _bacc
    from concourse import mybir as _mybir
    from concourse.bass_utils import run_bass_kernel_spmd as _run

    nc = _bacc.Bacc("TRN2", target_bir_lowering=False, num_devices=1)
    arrays, args = {}, []
    for name in _INS:
        a = _np.ascontiguousarray(inputs[name])
        arrays[f"in_{name}"] = a
        args.append(nc.dram_tensor(f"in_{name}", a.shape, _mybir.dt.from_np(a.dtype), kind="ExternalInput").ap())
    x = inputs["L0_attn_x"]
    args.append(nc.dram_tensor("out_x", x.shape, _mybir.dt.from_np(_np.dtype(x.dtype)), kind="ExternalOutput").ap())
    build_macaron(nc, *args)
    r = _run(nc, [arrays], core_ids=[0])
    return r.results[0]["out_x"]
```

```python
import concourse.bass as bass
from concourse import mybir
from contextlib import ExitStack
from collections import deque

F32 = mybir.dt.float32
BF16 = mybir.dt.bfloat16
I32 = mybir.dt.int32
ALU = mybir.AluOpType
ACT = mybir.ActivationFunctionType
AX = mybir.AxisListType


class Token:

    def __init__(self, sem, value):
        self.sem, self.value = sem, value


class Queue:

    def __init__(self, engine, sem):
        self.engine, self.sem, self.count, self.items, self.seen = engine, sem, 0, [], {}

    def wait(self, *tokens):
        for token in tokens:
            if token is not None and self.seen.get(id(token.sem), 0) < token.value:
                self.seen[id(token.sem)] = token.value
                self.items.append((self.engine.wait_ge, (token.sem, token.value), {}, None))

    def do(self, op, /, *args, **kwargs):
        self.items.append((op, args, kwargs, None))

    def mark(self, op, /, *args, **kwargs):
        self.count += 1
        self.items.append((op, args, kwargs, (self.sem, 1)))
        return Token(self.sem, self.count)

    def then(self, op, /, *args, **kwargs):
        token = self.mark(op, *args, **kwargs)
        self.wait(token)
        return token

    def dma(self, lane, out, in_):
        lane.count += 16
        self.items.append((self.engine.dma_start, (out, in_), {}, (lane.sem, 16)))
        return Token(lane.sem, lane.count)

    def counted(self, lane, issue):
        lane.count += 16
        self.items.append((issue, (), {}, (lane.sem, 16)))
        return Token(lane.sem, lane.count)

    def scatter(self, lane, out, rows, in_, **kwargs):
        lane.count += 16
        self.items.append((self.engine.indirect_dma_start,
                           (out, bass.IndirectOffsetOnAxis(ap=rows, axis=0), in_, None), kwargs, (lane.sem, 16)))
        return Token(lane.sem, lane.count)

    def play(self):
        for op, args, kwargs, inc in self.items:
            instruction = op(*args, **kwargs)
            if inc:
                instruction.then_inc(*inc)


class Lane:

    def __init__(self, sem):
        self.sem, self.count = sem, 0


def build_macaron(nc, x, w_qkv, w_o, ln_g, ln_b, router_w, eg, eb, w1, b1, w2, b2, wo, bo, out):
    P = 128
    B, N, F = x.shape
    E, D, H = w1.shape
    HEADS = 16
    DH = F // HEADS
    SCALE = 1.0 / float(DH) ** 0.5
    EPS = 1e-5
    TOPK = 2
    SETS, STAGGER = 2, 12
    HC = H // P
    BT = N // P
    T = B * BT
    TOKENS = B * N
    X2_LIMIT, LIMIT = 20.0, 10000.0

    W1, W2, WO = 0, H, 2 * H
    BIAS1, BIAS2, CLIP_LO, CLIP_HI = (3 * H + k * HC for k in range(4))
    BO = 3 * H + 4 * HC
    RECORD = BO + F

    GATE, NUMBER, ROW = F, F + 1, F + 2
    BLOCK = 2 * P
    BH = BLOCK // P
    REGION = TOKENS + BLOCK
    BLOCKS = (TOPK * TOKENS - E) // BLOCK + E
    SLOTS = 6

    stack = ExitStack()
    with stack:
        def sbuf(name, shape, dt=F32, owner=stack):
            return owner.enter_context(nc.sbuf_tensor(name, shape, dt))

        def semaphore(name):
            return stack.enter_context(nc.semaphore(name))

        pe = Queue(nc.tensor, semaphore("pe_done"))
        act = Queue(nc.scalar, semaphore("act_done"))
        dve = Queue(nc.vector, semaphore("dve_done"))
        pool = Queue(nc.gpsimd, semaphore("pool_done"))
        sp = Queue(nc.sync, semaphore("sp_done"))
        V, G, S, TE = nc.vector, nc.gpsimd, nc.scalar, nc.tensor

        x_sb = sbuf("x_sb", [P, T, F])
        record = sbuf("record", [P, E, RECORD])
        ln_g_bc = sbuf("ln_g_bc", [P, F])
        ln_b_bc = sbuf("ln_b_bc", [P, F])
        router_sb = sbuf("router_sb", [P, E])
        identity = sbuf("identity", [P, P])
        before = sbuf("before", [P, P], BF16)
        ones = sbuf("ones", [P, P], BF16)
        earlier = sbuf("earlier", [P, E, E])
        minus_half = sbuf("minus_half", [P, 1])
        number = sbuf("number", [P, T])
        region = sbuf("region", [P, E])
        block_f = sbuf("block_f", [1, BLOCKS])
        unit = sbuf("unit", [1, E])
        tiles_i = sbuf("tiles_i", [1, E], I32)
        tiles_f = sbuf("tiles_f", [1, E])
        tiles_end = sbuf("tiles_end", [1, E])
        tiles_start = sbuf("tiles_start", [1, E])
        end_f = sbuf("end_f", [1, E])
        end_i = sbuf("end_i", [1, E], I32)
        passed = sbuf("passed", [1, BLOCKS, E + 1])
        within = sbuf("within", [1, BLOCKS, E])
        local = sbuf("local", [1, BLOCKS])
        whose = sbuf("whose", [1, 2, BLOCKS])
        whose_i = sbuf("whose_i", [1, 2, BLOCKS], I32)
        wqkv_t = sbuf("wqkv_t", [P, P])
        wo_t = sbuf("wo_t", [P, P])

        class Set:

            def __init__(self, k, owner):
                def buf(name, shape, dt=F32):
                    return sbuf(f"{name}{k}", shape, dt, owner)

                self.stats = buf("stats", [P, BT, 6])
                self.mean_var = buf("mean_var", [P, BT, 2])
                self.shifted = buf("shifted", [P, BT])
                self.rstd = buf("rstd", [P, BT])
                self.xf = buf("xf", [P, BT, F])
                self.xf_t = buf("xf_t", [P, N])
                self.rows = buf("rows", [P, BT, TOPK, ROW])
                self.logits = buf("logits", [P, BT, E])
                self.ties = buf("ties", [P, BT, E, E])
                self.wins = buf("wins", [P, BT, E, E])
                self.rank = buf("rank", [P, BT, E])
                self.is_top = buf("is_top", [P, TOPK, BT, E])
                self.picked = buf("picked", [P, TOPK, BT, E])
                self.top = buf("top", [P, TOPK, BT])
                self.ratio = buf("ratio", [P, BT])
                self.chosen = buf("chosen", [P, BT, E], BF16)
                self.tallies = buf("tallies", [P, 2, BT, E])
                self.counts = buf("counts", [P, BT + 1, E])
                self.place = buf("place", [P, BT, E])
                self.place_f = buf("place_f", [P, TOPK, BT])
                self.place_i = buf("place_i", [P, TOPK, BT], I32)
                self.scattered = ()
                self.lanes = [Lane(semaphore(f"rows_out{k}_{j}")) for j in range(TOPK)]

        sets = [Set(0, stack)]

        bank = [stack.enter_context(nc.psum_tensor(f"bank{i}", [P, 512], F32)) for i in range(4)]
        wide = [stack.enter_context(nc.psum_tensor(f"wide{i}", [P, 1024], F32)) for i in range(2)]

        rows_dram = [nc.dram_tensor(f"rows{k}_dram", [E * REGION + BLOCK, ROW], F32) for k in range(2)]
        filler_dram = nc.dram_tensor("filler_dram", [BLOCK, ROW], F32)
        sum_dram = [nc.dram_tensor(f"sum{k}_dram", [TOKENS + BLOCK, F], F32) for k in range(2)]

        lane_x = [Lane(semaphore(f"x_in{b}")) for b in range(B)]
        lane_const = Lane(semaphore("const_in"))
        lane_w = [Lane(semaphore(f"expert_in{e}")) for e in range(E)]
        lane_sum = Lane(semaphore("x_into_sum"))
        lane_filler = Lane(semaphore("filler_made"))
        lane_fill = [Lane(semaphore(f"filler_out{k}")) for k in range(2)]
        lane_block = [Lane(semaphore(f"block_in{k}")) for k in range(SLOTS)]
        lane_add = [Lane(semaphore(f"added{k}")) for k in range(BH)]
        lane_out = Lane(semaphore("out_written"))

        wide_free, taken = [None, None], [0]

        def take_wide():
            n = taken[0] % 2
            taken[0] += 1
            pe.wait(wide_free[n])
            return n

        class Side:
            banks, turn, free, held = [0, 1, 2, 3], 0, {}, 0

        def take_bank():
            n = Side.banks[Side.turn % len(Side.banks)]
            Side.turn += 1
            Side.held += 1
            assert Side.free.get(n, None) != "held"
            pe.wait(Side.free.get(n))
            Side.free[n] = "held"
            return n

        def give_bank(n, token):
            Side.held -= 1
            Side.free[n] = token
            return token

        def batch_rows(tensor, b):
            return tensor[b * N:(b + 1) * N, :].rearrange("(p t) f -> p t f", p=P)

        def batch(b):
            return x_sb[:, b * BT:(b + 1) * BT, :]

        first = ExitStack()
        sets.extend(Set(k, first) for k in range(1, SETS))
        VEC = 2 * E + 2 * E * HC
        vec_rows = sbuf("vec_rows", [VEC, P], owner=first)
        vecs = sbuf("vecs", [P, VEC], owner=first)
        eg_col, eb_col = vecs[:, 0:E], vecs[:, E:2 * E]
        b_col = [vecs[:, 2 * E:2 * E + E * HC], vecs[:, 2 * E + E * HC:VEC]]

        x_rows = x.rearrange("b n f -> (b n) f")
        out_rows = out.rearrange("b n f -> (b n) f")
        x_in = {b: sp.dma(lane_x[b], batch(b), batch_rows(x_rows, b)) for b in range(B)}
        sp.dma(lane_const, ln_g_bc[:, :], ln_g.unsqueeze(0).to_broadcast([P, F]))
        sp.dma(lane_const, ln_b_bc[:, :], ln_b.unsqueeze(0).to_broadcast([P, F]))
        sp.dma(lane_const, router_sb[:, :], router_w)
        sp.dma(lane_const, vec_rows[0:E, :], eg)
        sp.dma(lane_const, vec_rows[E:2 * E, :], eb)
        sp.dma(lane_const, vec_rows[2 * E:2 * E + E * HC, :], b1.rearrange("e (c p) -> (e c) p", p=P))
        sp.dma(lane_const, vec_rows[2 * E + E * HC:VEC, :], b2.rearrange("e (c p) -> (e c) p", p=P))
        const_in = sp.dma(lane_const, record[:, :, BO:BO + F], bo.unsqueeze(0).to_broadcast([P, E, F]))
        expert_in = []
        for e in range(E):
            sp.dma(lane_w[e], record[:, e, W1:W1 + H], w1[e])
            sp.dma(lane_w[e], record[:, e, W2:W2 + H], w2[e])
            expert_in.append(sp.dma(lane_w[e], record[:, e, WO:WO + H].rearrange("p (c d) -> p c d", d=F),
                                    wo[e].rearrange("(c p) d -> p c d", p=P)))
        x_in_sum = sp.dma(lane_sum, sum_dram[0][0:TOKENS, :], x_rows)

        pool.then(G.memset, identity[:, :], 0.0)
        identity_made = pool.then(G.affine_select, out=identity[:, :], in_=identity[:, :],
                                  compare_op=ALU.not_equal, fill=1.0, base=0,
                                  pattern=[[-1, P]], channel_multiplier=1)
        pool.do(G.memset, minus_half[:, :], -0.5)
        pool.do(G.memset, ones[:, :], 1.0)
        pool.then(G.memset, before[:, :], 1.0)
        pool.do(G.affine_select, out=before[:, :], in_=before[:, :], compare_op=ALU.is_gt, fill=0.0,
                base=0, pattern=[[1, P]], channel_multiplier=-1)
        pool.then(G.memset, earlier[:, :, :], 1.0)
        pool.do(G.affine_select, out=earlier[:, :, :], in_=earlier[:, :, :], compare_op=ALU.is_gt,
                fill=0.0, base=0, pattern=[[1, E], [-1, E]], channel_multiplier=0)
        numbering = sbuf("numbering", [P, T], I32, first)
        regions = sbuf("regions", [P, E], I32, first)
        blocks_i = sbuf("blocks_i", [1, BLOCKS], I32, first)
        spares_i = sbuf("spares_i", [P, BH], I32, first)
        filler = sbuf("filler", [P, BH, ROW], owner=first)
        pool.do(G.iota, numbering[:, :], pattern=[[N, B], [1, BT]], base=0, channel_multiplier=BT)
        pool.do(G.iota, regions[:, :], pattern=[[REGION, E]], base=0, channel_multiplier=0)
        pool.do(G.iota, blocks_i[:, :], pattern=[[1, BLOCKS]], base=0, channel_multiplier=0)
        pool.do(G.iota, spares_i[:, :], pattern=[[1, BH]], base=TOKENS, channel_multiplier=BH)
        pool.do(G.memset, unit[:, :], 1.0)
        counted = pool.mark(G.memset, filler[:, :, :], 0.0)
        dve.wait(counted)
        dve.do(V.tensor_copy, number[:, :], numbering[:, :])
        dve.do(V.tensor_copy, region[:, :], regions[:, :])
        dve.do(V.tensor_copy, block_f[:, :], blocks_i[:, :])
        constants_made = dve.then(V.tensor_copy, filler[:, :, NUMBER], spares_i[:, :])
        sp.wait(constants_made)
        filler_made = sp.dma(lane_filler, filler_dram[:, :].rearrange("(p r) c -> p r c", r=BH), filler[:, :, :])
        sp.wait(filler_made)
        for k in range(2):
            sp.dma(lane_fill[k], rows_dram[k][E * REGION:E * REGION + BLOCK, :], filler_dram[:, :])

        folded = []

        def fold_expert_vectors():
            vec_bank = wide[0][:, 0:VEC]
            bias_bank = [wide[1][:, k * 512:k * 512 + E * HC] for k in range(2)]
            pe.wait(const_in, identity_made)
            turned = pe.mark(TE.transpose, vec_bank, vec_rows[:, :], identity[0:VEC, 0:VEC])
            act.wait(turned)
            copied = wide_free[0] = act.mark(S.copy, vecs[:, :], vec_bank)
            act.wait(copied)
            pe.wait(copied)
            yield
            for e in range(E):
                pe.wait(expert_in[e])
                for k, w in enumerate((W1, W2)):
                    for c in range(HC):
                        last = pe.mark(TE.matmul, bias_bank[k][:, e * HC + c:e * HC + c + 1],
                                       record[:, e, w + c * P:w + (c + 1) * P], eb_col[:, e:e + 1],
                                       start=True, stop=True)
                act.wait(last)
                both = record[:, e, W1:W1 + 2 * H]
                scaled = act.mark(S.activation, both, both, ACT.Copy, scale=eg_col[:, e:e + 1])
                yield
            bias = [record[:, :, at:at + HC] for at in (BIAS1, BIAS2)]
            dve.wait(last, copied)
            for k in range(2):
                wide_free[1] = dve.then(V.tensor_tensor, bias[k], bias_bank[k].rearrange("p (e c) -> p e c", c=HC),
                                        b_col[k].rearrange("p (e c) -> p e c", c=HC), ALU.add)
            dve.do(V.tensor_scalar, record[:, :, CLIP_LO:CLIP_LO + HC], bias[1], -1.0, -X2_LIMIT,
                   ALU.mult, ALU.add)
            folded[:] = [scaled, dve.then(V.tensor_scalar, record[:, :, CLIP_HI:CLIP_HI + HC], bias[1], -1.0,
                                          X2_LIMIT, ALU.mult, ALU.add)]

        def row_statistics(src, nt, r):
            for t in range(nt):
                last = dve.mark(V.bn_stats, out=r.stats[:, t, :], in_=src[:, t, :])
                if t % 2:
                    yield
            dve.wait(last)
            for t in range(nt):
                last = dve.mark(V.bn_aggr, out=r.mean_var[:, t, :], in_=r.stats[:, t, :])
                if t == nt // 2:
                    yield
            dve.wait(last)

        def inverse_deviation(r, nt, scale=1.0, shift=EPS):
            ready = dve.mark(V.tensor_scalar, r.shifted[:, 0:nt], r.mean_var[:, 0:nt, 1], scale, shift,
                             ALU.mult, ALU.add)
            pool.wait(ready)
            return pool.mark(G.tensor_tensor, r.rstd[:, 0:nt], r.shifted[:, 0:nt],
                             minus_half[:, 0:1].to_broadcast([P, nt]), ALU.pow)

        def pause(mill, steps):
            for _ in range(steps if mill[0] is pool else 0):
                yield

        def turn_tiles(dst, tiles, nt, ready):
            for at in range(0, nt, 4):
                n = take_bank()
                pe.wait(ready, identity_made)
                for t in range(4):
                    last = pe.mark(TE.transpose, bank[n][:, t * P:(t + 1) * P], tiles[:, at + t, :],
                                   identity[:, :])
                yield
                act.wait(last)
                turned = give_bank(n, act.mark(S.copy, dst[:, at * P:(at + 4) * P], bank[n][:, :]))
                yield
            return turned

        def route(k_ffn, b, r, mill, t0=0, nt=BT):
            mq, M = mill
            src = x_sb[:, b * BT + t0:b * BT + t0 + nt, :]
            few = slice(0, nt)
            dve.wait(x_in.get(b))
            yield from row_statistics(src, nt, r)
            ready = inverse_deviation(r, nt, 1.0 + EPS, EPS * EPS)
            yield from pause(mill, 2)
            mq.wait(const_in, ready)
            for t in range(nt):
                last = mq.mark(M.tensor_scalar, r.xf[:, t, :], src[:, t, :], r.mean_var[:, t, 0:1],
                               r.rstd[:, t:t + 1], ALU.subtract, ALU.mult)
            mq.wait(last)
            yield
            xf = r.xf[:, few, :]
            mq.then(M.tensor_tensor, xf, xf, ln_g_bc[:, :].unsqueeze(1).to_broadcast([P, nt, F]), ALU.mult)
            yield
            xf_ready = mq.mark(M.tensor_tensor, xf, xf, ln_b_bc[:, :].unsqueeze(1).to_broadcast([P, nt, F]), ALU.add)
            yield from pause(mill, 22)
            yield
            xf_t_ready = yield from turn_tiles(r.xf_t, r.xf, nt, xf_ready)
            n = take_bank()
            pe.wait(xf_t_ready)
            for t in range(nt):
                last = pe.mark(TE.matmul, bank[n][:, t * E:(t + 1) * E], r.xf_t[:, t * P:(t + 1) * P],
                               router_sb[:, :], start=True, stop=True)
            yield
            act.wait(last)
            scored = give_bank(n, act.mark(S.copy, r.logits[:, few, :],
                                           bank[n][:, 0:nt * E].rearrange("p (t e) -> p t e", e=E)))
            dve.wait(xf_ready)
            yield from row_statistics(r.xf, nt, r)
            ready = inverse_deviation(r, nt)
            yield from pause(mill, 2)
            shape = [P, nt, E, E]
            theirs = r.logits[:, few, :].unsqueeze(2).to_broadcast(shape)
            mine = r.logits[:, few, :].unsqueeze(3).to_broadcast(shape)
            dve.wait(constants_made, scored)
            dve.do(V.tensor_tensor, r.wins[:, few, :, :], theirs, mine, ALU.is_gt)
            yield
            dve.then(V.tensor_tensor, r.ties[:, few, :, :], theirs, mine, ALU.is_equal)
            yield
            dve.then(V.tensor_tensor, r.ties[:, few, :, :], r.ties[:, few, :, :],
                    earlier[:, :, :].unsqueeze(1).to_broadcast(shape), ALU.mult)
            yield
            dve.then(V.tensor_tensor, r.wins[:, few, :, :], r.wins[:, few, :, :], r.ties[:, few, :, :],
                     ALU.add)
            mq.wait(ready, *r.scattered)
            for t in range(nt):
                filled = mq.mark(M.tensor_scalar, r.rows[:, t, :, 0:F],
                                 r.xf[:, t, :].unsqueeze(1).to_broadcast([P, TOPK, F]),
                                 r.mean_var[:, t, 0:1], r.rstd[:, t:t + 1], ALU.subtract, ALU.mult)
            yield from pause(mill, 14)
            dve.then(V.tensor_reduce, out=r.rank[:, few, :], in_=r.wins[:, few, :, :], axis=AX.X, op=ALU.add)
            for k in range(TOPK):
                last = dve.mark(V.tensor_scalar, r.is_top[:, k, few, :], r.rank[:, few, :], float(k), None,
                                ALU.is_equal)
            dve.wait(last)
            chosen_ready = dve.mark(V.tensor_tensor, r.chosen[:, few, :], r.is_top[:, 0, few, :], r.is_top[:, 1, few, :],
                                    ALU.add)
            yield
            n = take_bank()
            pe.wait(chosen_ready)
            flat = r.chosen[:, few, :].rearrange("p t e -> p (t e)")
            pe.do(TE.matmul, bank[n][:, 0:nt * E], before[:, :], flat, start=True, stop=True)
            tallied = pe.mark(TE.matmul, bank[n][:, nt * E:2 * nt * E], ones[:, :], flat, start=True, stop=True)
            dve.then(V.tensor_tensor, r.picked[:, :, few, :], r.is_top[:, :, few, :],
                     r.logits[:, few, :].unsqueeze(1).to_broadcast([P, TOPK, nt, E]), ALU.mult)
            dve.then(V.tensor_reduce, out=r.top[:, :, few], in_=r.picked[:, :, few, :], axis=AX.X, op=ALU.add)
            led = dve.mark(V.tensor_tensor, r.ratio[:, few], r.top[:, 1, few], r.top[:, 0, few], ALU.subtract)
            yield
            act.wait(led, tallied)
            shared = act.mark(S.activation, r.ratio[:, few], r.ratio[:, few], ACT.Exp)
            tallies_in = give_bank(n, act.mark(S.copy, r.tallies[:, :, few, :],
                                               bank[n][:, 0:2 * nt * E].rearrange("p (k t e) -> p k t e", k=2, e=E)))
            yield
            total = running[0]
            running[0] = r.counts[:, nt, :]
            dve.wait(tallies_in)
            if total is None:
                dve.then(V.memset, r.counts[:, 0, :], 0.0)
            else:
                dve.then(V.tensor_copy, r.counts[:, 0, :], total)
            for t in range(nt):
                dve.then(V.tensor_tensor, r.counts[:, t + 1, :], r.counts[:, t, :], r.tallies[:, 1, t, :], ALU.add)
                if t % 4 == 3:
                    yield
            yield
            dve.then(V.tensor_tensor, r.place[:, few, :], r.tallies[:, 0, few, :], r.counts[:, few, :], ALU.add)
            dve.then(V.tensor_tensor, r.place[:, few, :], r.place[:, few, :],
                     region[:, :].unsqueeze(1).to_broadcast([P, nt, E]), ALU.add)
            dve.then(V.tensor_tensor, r.picked[:, :, few, :], r.is_top[:, :, few, :],
                     r.place[:, few, :].unsqueeze(1).to_broadcast([P, TOPK, nt, E]), ALU.mult)
            dve.then(V.tensor_reduce, out=r.place_f[:, :, few], in_=r.picked[:, :, few, :], axis=AX.X, op=ALU.add)
            dve.wait(*r.scattered)
            dve.do(V.tensor_copy, r.place_i[:, :, few], r.place_f[:, :, few])
            yield
            dve.wait(shared)
            dve.then(V.tensor_scalar, r.top[:, 0, few], r.ratio[:, few], 1.0, None, ALU.add)
            dve.then(V.reciprocal, r.top[:, 1, few], r.top[:, 0, few])
            dve.wait(filled)
            dve.do(V.tensor_copy, r.rows[:, few, 0, GATE], r.top[:, 1, few])
            dve.do(V.tensor_tensor, r.rows[:, few, 1, GATE], r.ratio[:, few], r.top[:, 1, few], ALU.mult)
            placed = dve.then(V.tensor_copy, r.rows[:, few, :, NUMBER],
                              number[:, b * BT + t0:b * BT + t0 + nt].unsqueeze(2).to_broadcast([P, nt, TOPK]))
            yield
            pool.wait(placed)
            out_now = [None] * TOPK
            for t in range(nt):
                for k in range(TOPK):
                    out_now[k] = pool.scatter(r.lanes[k], rows_dram[k_ffn][:, :], r.place_i[:, k, t:t + 1],
                                              r.rows[:, t, k, :])
                if t % 2:
                    yield
            r.scattered = tuple(out_now)
            rows_written[k_ffn].extend(out_now)

        running = [None]
        rows_written = [[], []]

        def lay_out_blocks(k_ffn):
            total = running[0][0:1, :]
            running[0] = None
            dve.then(V.tensor_tensor, end_f[:, :], total, region[0:1, :], ALU.add)
            placed = dve.then(V.tensor_copy, end_i[:, :], end_f[:, :])
            sp.wait(placed)

            def fill_after(e):
                def issue():
                    row = nc.sync.value_load(end_i[0:1, e:e + 1], min_val=0, max_val=E * REGION)
                    return nc.sync.dma_start(rows_dram[k_ffn][bass.ds(row, BLOCK), :], filler_dram[:, :])
                return issue

            for e in range(E):
                filled = sp.counted(lane_fill[k_ffn], fill_after(e))

            dve.then(V.tensor_scalar, tiles_f[:, :], total, float(BLOCK - 1), None, ALU.add)
            dve.then(V.tensor_copy, tiles_i[:, :], tiles_f[:, :])
            dve.then(V.tensor_scalar, tiles_i[:, :], tiles_i[:, :], BLOCK.bit_length() - 1, None,
                     ALU.logical_shift_right)
            dve.then(V.tensor_copy, tiles_f[:, :], tiles_i[:, :])
            dve.then(V.tensor_tensor_scan, tiles_end[:, :], unit[:, :], tiles_f[:, :], 0.0, ALU.mult, ALU.add)
            dve.then(V.tensor_tensor, tiles_start[:, :], tiles_end[:, :], tiles_f[:, :], ALU.subtract)
            shape = [1, BLOCKS, E]
            blocks = block_f[:, :].unsqueeze(2).to_broadcast(shape)
            dve.do(V.memset, passed[:, :, 0:1], 1.0)
            dve.do(V.tensor_tensor, passed[:, :, 1:E + 1], blocks,
                   tiles_end[:, :].unsqueeze(1).to_broadcast(shape), ALU.is_ge)
            dve.then(V.tensor_tensor, within[:, :, :], blocks,
                     tiles_start[:, :].unsqueeze(1).to_broadcast(shape), ALU.subtract)
            dve.then(V.tensor_reduce, out=whose[:, 0, :], in_=passed[:, :, 1:E + 1], axis=AX.X, op=ALU.add)
            dve.then(V.tensor_tensor, passed[:, :, 0:E], passed[:, :, 0:E], passed[:, :, 1:E + 1], ALU.subtract)
            dve.then(V.tensor_tensor, within[:, :, :], within[:, :, :], passed[:, :, 0:E], ALU.mult)
            dve.then(V.tensor_reduce, out=local[:, :], in_=within[:, :, :], axis=AX.X, op=ALU.add)
            dve.do(V.tensor_scalar, whose[:, 1, :], whose[:, 0, :], float(REGION), None, ALU.mult)
            dve.then(V.tensor_scalar, local[:, :], local[:, :], float(BLOCK), None, ALU.mult)
            dve.do(V.tensor_tensor, whose[:, 1, :], whose[:, 1, :], local[:, :], ALU.add)
            dve.then(V.tensor_scalar, whose[:, 0, :], whose[:, 0, :], float(E - 1), None, ALU.min)
            return filled, dve.then(V.tensor_copy, whose_i[:, :, :], whose[:, :, :])

        def experts(k_ffn, start):
            own = ExitStack()

            def buf(name, shape, dt=F32):
                return sbuf(f"ffn{k_ffn}_{name}", shape, dt, own)

            filled, known = lay_out_blocks(k_ffn)

            for q in (dve, pool, act, pe, sp):
                q.wait(*start)
            rec = buf("rec", [P, SLOTS, RECORD])
            block_rows = buf("block_rows", [P, SLOTS, BH, ROW])
            block_t = buf("block_t", [P, 2, BLOCK])
            x2c = buf("x2c", [P, 2, BLOCK])
            silu = buf("silu", [P, 2, BLOCK])
            hidden = buf("hidden", [P, 2, HC, BLOCK])
            y = buf("y", [P, 2, BH, F])
            number_i = buf("number_i", [P, 2, BH], I32)

            chunk_bank = [bank[0], bank[1], bank[2], wide[0][:, 0:512]]
            y_bank = [bank[3][:, 0:BLOCK], wide[1][:, 0:BLOCK]]
            turn_bank = [wide[0][:, 512:512 + BLOCK], wide[1][:, 512:512 + BLOCK]]
            chunk_free = [None] * 4
            y_free, turn_free = [None, None], [None, None]
            hidden_free, hidden_ready, turned_ready = [None, None], {}, {}
            block_in, slot_free = {}, {}
            block_t_free = [None, None]
            silu_done = {}
            added = {}
            product = {}

            def load_block(i):
                s = i % SLOTS
                sp.wait(known, filled, *rows_written[k_ffn], *folded, *slot_free.get(i - SLOTS, ()))

                def record_in():
                    expert = nc.sync.value_load(whose_i[0:1, 0, i:i + 1], min_val=0, max_val=E - 1)
                    return nc.sync.dma_start(rec[:, s, :].unsqueeze(1), record[:, bass.ds(expert, 1), :])

                def rows_in():
                    row = nc.sync.value_load(whose_i[0:1, 1, i:i + 1], min_val=0, max_val=E * REGION)
                    return nc.sync.dma_start(block_rows[:, s, :, :],
                                             rows_dram[k_ffn][bass.ds(row, BLOCK), :]
                                             .rearrange("(p r) c -> p r c", r=BH))

                sp.counted(lane_block[s], rows_in)
                block_in[i] = sp.counted(lane_block[s], record_in)

            def turn(i):
                s = i % SLOTS
                pe.wait(block_in[i], turn_free[i % 2])
                for r in range(BH):
                    last = pe.mark(TE.transpose, turn_bank[i % 2][:, r * P:(r + 1) * P],
                                   block_rows[:, s, r, 0:F], identity[:, :])
                act.wait(last, block_t_free[i % 2])
                turned_ready[i] = turn_free[i % 2] = act.mark(S.copy, block_t[:, i % 2, :], turn_bank[i % 2])

            def combine(item):
                i, c, n = item
                s = i % SLOTS
                dve.wait(silu_done[n], hidden_free[i % 2])
                chunk_free[n % 4] = dve.mark(
                    V.scalar_tensor_tensor, hidden[:, i % 2, c, :], chunk_bank[n % 4][:, BLOCK:2 * BLOCK],
                    rec[:, s, BIAS1 + c:BIAS1 + c + 1], silu[:, n % 2, :], ALU.add, ALU.mult)
                if c == HC - 1:
                    dve.wait(chunk_free[n % 4])
                    hidden_ready[i] = dve.mark(V.tensor_scalar, hidden[:, i % 2, :, :], hidden[:, i % 2, :, :],
                                               LIMIT, -LIMIT, ALU.min, ALU.max)

            def second_product(i):
                s = i % SLOTS
                pe.wait(hidden_ready[i], y_free[i % 2])
                for r in range(BH):
                    for c in range(HC):
                        last = (pe.mark if (r, c) == (BH - 1, HC - 1) else pe.do)(
                            TE.matmul, y_bank[i % 2][:, r * F:(r + 1) * F],
                            hidden[:, i % 2, c, r * P:(r + 1) * P], rec[:, s, WO + c * F:WO + (c + 1) * F],
                            start=(c == 0), stop=(c == HC - 1))
                hidden_free[i % 2] = product[i] = last

            def add_block(i):
                s = i % SLOTS
                mine = y[:, i % 2, :, :]
                dve.wait(product[i], *added.get(i - 2, ()))
                y_free[i % 2] = dve.then(
                    V.tensor_tensor, mine, y_bank[i % 2].rearrange("p (r f) -> p r f", f=F),
                    rec[:, s, BO:BO + F].unsqueeze(1).to_broadcast([P, BH, F]), ALU.add)
                dve.then(V.tensor_scalar, mine, mine, LIMIT, -LIMIT, ALU.min, ALU.max)
                dve.do(V.tensor_copy, number_i[:, i % 2, :], block_rows[:, s, :, NUMBER])
                for r in range(BH):
                    weighed = dve.mark(V.tensor_scalar, mine[:, r, :], mine[:, r, :],
                                       block_rows[:, s, r, GATE:GATE + 1], 0.5, ALU.mult, ALU.mult)
                slot_free[i] = (weighed, product[i])
                pool.wait(weighed, x_in_sum_of[k_ffn], *added.get(i - 1, ()))
                added[i] = [pool.scatter(lane_add[r], sum_dram[k_ffn][:, :], number_i[:, i % 2, r:r + 1],
                                         mine[:, r, :], compute_op=ALU.add) for r in range(BH)]

            for i in range(SLOTS):
                load_block(i)
            turn(0)
            waiting, n = None, 0
            for i in range(BLOCKS):
                s = i % SLOTS
                pe.wait(turned_ready[i])
                for c in range(HC):
                    both = chunk_bank[n % 4]
                    pe.wait(chunk_free[n % 4])
                    pe.do(TE.matmul, both[:, 0:BLOCK], rec[:, s, W2 + c * P:W2 + (c + 1) * P],
                          block_t[:, i % 2, :], start=True, stop=True)
                    last = pe.mark(TE.matmul, both[:, BLOCK:2 * BLOCK], rec[:, s, W1 + c * P:W1 + (c + 1) * P],
                                   block_t[:, i % 2, :], start=True, stop=True)
                    dve.wait(last, silu_done.get(n - 2))
                    clipped = dve.mark(V.tensor_scalar, x2c[:, n % 2, :], both[:, 0:BLOCK],
                                       rec[:, s, CLIP_LO + c:CLIP_LO + c + 1],
                                       rec[:, s, CLIP_HI + c:CLIP_HI + c + 1], ALU.max, ALU.min)
                    act.wait(clipped, chunk_free[(n - 2) % 4])
                    silu_done[n] = act.mark(S.activation, silu[:, n % 2, :], x2c[:, n % 2, :], ACT.Silu,
                                            bias=rec[:, s, BIAS2 + c:BIAS2 + c + 1])
                    if waiting:
                        combine(waiting)
                    waiting = (i, c, n)
                    n += 1
                    if c == 0 and i + 1 < BLOCKS:
                        turn(i + 1)
                    if c == 2 and i:
                        second_product(i - 1)
                        add_block(i - 1)
                        if i - 1 + SLOTS < BLOCKS:
                            load_block(i - 1 + SLOTS)
                block_t_free[i % 2] = last
            combine(waiting)
            second_product(BLOCKS - 1)
            add_block(BLOCKS - 1)
            own.close()
            return added[BLOCKS - 1] + [chunk_free[(n - 1) % 4], turned_ready[BLOCKS - 1], y_free[0], y_free[1],
                                        product[BLOCKS - 1], Token(dve.sem, dve.count), Token(act.sem, act.count)]

        def attention(start):
            own = ExitStack()

            def buf(name, shape, dt=F32):
                return sbuf(f"att_{name}", shape, dt, own)

            PARTS = 3
            ROWS = DH * PARTS * PARTS
            MROWS = -(-ROWS // 32) * 32
            KROWS = MROWS + PARTS
            TEAM = 4
            TEAMS = HEADS // TEAM
            HALF = N // 2
            HT = HALF // P
            SLOTS = 3
            VS = P // TEAM
            VW = VS // 2
            NTEAM = B * TEAMS

            xh = buf("xh", [P, BT, F])
            q_t = buf("q_t", [P, N])
            rest = xh[:, :, :].rearrange("p t f -> p (t f)")
            attn_t = xh_t = buf("xh_t", [P, N])
            parts = buf("parts", [P, PARTS, N], BF16)
            left = buf("left", [P, SLOTS, TEAM, N], BF16)
            right = buf("right", [P, SLOTS, TEAM, N], BF16)
            values = buf("values", [P, 2, BT, HEADS, VW])
            neg_max = buf("neg_max", [P, 2, TEAM, BT])
            max_rest = buf("max_rest", [TEAM * BT, P])
            max_parts = buf("max_parts", [TEAM * BT, 2, PARTS, P], BF16)
            PROBS = 2 * TEAM
            probs = buf("probs", [P, PROBS, HALF])
            o_t = buf("o_t", [P, 2, HALF])
            inv_sum = buf("inv_sum", [P, HT, TEAM])
            attn = buf("attn", [P, BT, F])
            q_dram = nc.dram_tensor("q_parts_dram", [B, P, PARTS, N], BF16)
            q_copies_dram = nc.dram_tensor("q_copies_dram", [B, PARTS, P, PARTS, N], BF16)
            max_dram = nc.dram_tensor("max_parts_dram", [NTEAM, TEAM * BT, PARTS, P], BF16)

            lane_max_out = Lane(semaphore("max_parts_out"))
            lane_q = Lane(semaphore("q_parts_out"))
            lane_lr = [Lane(semaphore(f"operands_in{s}")) for s in range(SLOTS)]
            lane_max = [Lane(semaphore(f"max_in{s}")) for s in range(SLOTS)]
            score_bank = bank[0:2]
            value_bank = bank[3]
            Side.banks, Side.free = [2], {}

            for queue in (dve, act, pool, pe, sp):
                queue.wait(*start)

            w_rows = [o_t[:, 0, 0:P], o_t[:, 0, P:2 * P]]
            lane_wa = Lane(semaphore("attention_weights_in"))
            sp.dma(lane_wa, w_rows[0], w_qkv)
            weights_in = sp.dma(lane_wa, w_rows[1], w_o)
            n = take_wide()
            pe.wait(weights_in)
            pe.do(TE.transpose, wide[n][:, 0:P], w_rows[0], identity[:, :])
            last = pe.mark(TE.transpose, wide[n][:, P:2 * P], w_rows[1], identity[:, :])
            act.wait(last)
            act.do(S.copy, wqkv_t[:, :], wide[n][:, 0:P])
            weights_turned = wide_free[n] = act.mark(S.copy, wo_t[:, :], wide[n][:, P:2 * P])

            blank = [None] * SLOTS

            def blank_slot(s):
                dve.do(V.memset, right[:, s, :, :], 0.0)
                cleared = dve.mark(V.memset, values[:, s, :, :, :], 0.0) if s < 2 else None
                if s < 2:
                    dve.wait(cleared)
                    values_blank[s] = dve.mark(V.memset, values[:, s, :, :, DH:DH + 1], 1.0)
                blank[s] = (Token(dve.sem, dve.count),
                            act.mark(S.copy, left[:, s, :, :].rearrange("p j n -> p (j n)"),
                                     ones[:, 0:1].to_broadcast([P, TEAM * N])))

            values_blank = [None, None]
            blank_slot(0)

            value_bank_blank = dve.mark(V.memset, value_bank[:, :], 0.0)

            q_out, values_ready, values_free = {}, {}, {}

            def prepare(b, mill):
                mq, M = mill
                r = sets[0]
                src = batch(b)
                dve.wait(x_in[b])
                yield from row_statistics(src, BT, r)
                ready = inverse_deviation(r, BT)
                yield
                mq.wait(ready)
                for t in range(BT):
                    normed = mq.mark(M.tensor_scalar, xh[:, t, :], src[:, t, :], r.mean_var[:, t, 0:1],
                                     r.rstd[:, t:t + 1], ALU.subtract, ALU.mult)
                yield from pause(mill, 20)
                turned = yield from turn_tiles(xh_t, xh, BT, normed)
                for h in range(2):
                    half = slice(h * HALF, (h + 1) * HALF)
                    n = take_bank()
                    pe.wait(turned, weights_turned)
                    last = pe.mark(TE.matmul, bank[n][:, :], wqkv_t[:, :], xh_t[:, half], start=True, stop=True)
                    yield
                    act.wait(last)
                    projected = give_bank(n, act.mark(S.copy, q_t[:, half], bank[n][:, :]))
                    yield
                mq.wait(projected, q_out.get(b - 1))
                mq.then(M.tensor_copy, parts[:, 0, :], q_t[:, :])
                mq.then(M.tensor_tensor, rest, q_t[:, :], parts[:, 0, :], ALU.subtract)
                mq.then(M.tensor_copy, parts[:, 1, :], rest)
                mq.then(M.tensor_tensor, rest, rest, parts[:, 1, :], ALU.subtract)
                split = mq.then(M.tensor_copy, parts[:, 2, :], rest)
                yield from pause(mill, 20)
                sp.wait(split)
                sp.dma(lane_q, q_dram[b], parts[:, :, :])
                for k in range(PARTS):
                    yield from pause(mill, 2)
                    q_out[b] = sp.dma(lane_q, q_copies_dram[b, k],
                                      parts[:, k:k + 1, :].to_broadcast([P, PARTS, N]))
                yield
                for h in range(2):
                    n = take_bank()
                    pe.wait(projected)
                    for t in range(HT):
                        at = (h * HT + t) * P
                        last = pe.mark(TE.transpose, bank[n][:, t * P:(t + 1) * P], q_t[:, at:at + P],
                                       identity[:, :])
                    yield
                    act.wait(last, values_free.get(b - 2), values_blank[b % 2])
                    kept = values[:, b % 2, h * HT:(h + 1) * HT, :, 0:DH].rearrange("p t h d -> p (t h) d")
                    values_in = give_bank(n, act.mark(S.copy, kept,
                                                      bank[n][:, :].rearrange("p (th d) -> p th d", d=DH)))
                    yield
                values_ready[b] = values_in

            operands_in, scores_done = {}, {}

            def load_operands(i):
                b, team = divmod(i, TEAMS)
                s = i % SLOTS
                sp.wait(q_out[b], *blank[s], scores_done.get(i - SLOTS))
                heads = slice(team * TEAM * DH, (team + 1) * TEAM * DH)
                for k in range(PARTS):
                    block = slice(k * DH * PARTS, (k + 1) * DH * PARTS)
                    for side, rows in ((left, q_dram[b, heads]), (right, q_copies_dram[b, k, heads])):
                        operands_in[i] = sp.dma(lane_lr[s], side[block, s, :, :],
                                                rows.rearrange("(h d) j n -> (d j) h n", d=DH))

            def row_max(i, j, t):
                n = take_wide()
                s = i % SLOTS
                pe.wait(operands_in[i])
                for h in range(2):
                    last = (pe.do, pe.mark)[h](
                        TE.matmul, wide[n][:, h * HALF:(h + 1) * HALF], left[0:MROWS, s, j, t * P:(t + 1) * P],
                        right[0:MROWS, s, j, h * HALF:(h + 1) * HALF], start=True, stop=True)
                    if h == 0:
                        yield
                dve.wait(last)
                wide_free[n] = dve.mark(V.tensor_reduce, out=neg_max[:, i % 2, j, t:t + 1], in_=wide[n][:, :],
                                        axis=AX.X, op=ALU.max, negate=True)
                if (j, t) == (TEAM - 1, BT - 1):
                    place_max(i, wide_free[n])
                yield

            max_in, max_out = {}, {}

            def place_max(i, reduced):
                n = take_wide()
                s = i % SLOTS
                pe.wait(reduced)
                turned = pe.mark(TE.transpose, wide[n][0:TEAM * BT, 0:P],
                                 neg_max[:, i % 2, :, :].rearrange("p j t -> p (j t)"), identity[:, :])
                mine = max_parts[:, i % 2, :, :]
                dve.wait(turned, max_out.get(i - 2))
                wide_free[n] = dve.then(V.tensor_copy, max_rest[:, :], wide[n][0:TEAM * BT, 0:P])
                for k in range(PARTS):
                    last = dve.then(V.tensor_copy, mine[:, k, :], max_rest[:, :])
                    if k < PARTS - 1:
                        dve.then(V.tensor_tensor, max_rest[:, :], max_rest[:, :], mine[:, k, :], ALU.subtract)
                sp.wait(last)
                max_out[i] = sp.dma(lane_max_out, max_dram[i], mine)
                sp.wait(max_out[i])
                for j in range(TEAM):
                    max_in[i] = sp.dma(lane_max[s], right[MROWS:KROWS, s, j, :].rearrange("k (t q) -> k t q", q=P),
                                       max_dram[i, j * BT:(j + 1) * BT, :, :].rearrange("t k q -> k t q"))

            urgent, background = deque(), deque()
            attn_free = [None, None]
            o_free = [None, None]
            value_free = [value_bank_blank]
            ended = []

            def finish_half(i, half, summed):
                b, team = divmod(i, TEAMS)
                act.wait(summed, o_free[half])
                copied = value_free[0] = act.mark(S.copy, o_t[:, half, :], value_bank[:, :])
                yield
                yield
                yield
                n = take_bank()
                pe.wait(copied)
                for t in range(HT):
                    last = pe.mark(TE.transpose, bank[n][:, t * P:(t + 1) * P],
                                   o_t[:, half, t * P:(t + 1) * P], identity[:, :])
                o_free[half] = last
                yield
                o = bank[n][:, 0:HT * P].rearrange("p (t j d) -> p t j d", t=HT, j=TEAM)
                dve.wait(last, attn_free[half])
                dve.then(V.reciprocal, inv_sum[:, :, :], o[:, :, :, DH])
                where = attn[:, half * HT:(half + 1) * HT, team * TEAM * DH:(team + 1) * TEAM * DH]
                placed = give_bank(n, dve.then(
                    V.tensor_tensor, where.rearrange("p t (j d) -> p t j d", j=TEAM), o[:, :, :, 0:DH],
                    inv_sum[:, :, :].unsqueeze(3).to_broadcast([P, HT, TEAM, DH]), ALU.mult))
                if team == TEAMS - 1:
                    urgent.append(finish_rows(b, half, placed))

            def finish_rows(b, half, placed):
                r = slice(half * HT, (half + 1) * HT)
                turned = yield from turn_tiles(attn_t[:, half * HALF:(half + 1) * HALF], attn[:, r, :], HT, placed)
                attn_free[half] = turned
                n = take_bank()
                pe.wait(turned)
                for t in range(HT):
                    at = (half * HT + t) * P
                    last = pe.mark(TE.matmul, bank[n][:, t * P:(t + 1) * P], attn_t[:, at:at + P],
                                   wo_t[:, :], start=True, stop=True)
                yield
                rows = batch(b)[:, r, :]
                dve.wait(last)
                x_in[b] = give_bank(n, dve.then(V.tensor_tensor, rows, rows,
                                                bank[n][:, :].rearrange("p (t f) -> p t f", f=F), ALU.add))
                if half == 1:
                    yield
                    sp.wait(x_in[b])
                    x_in_sum_of[1] = sp.dma(lane_sum, batch_rows(sum_dram[1], b), batch(b))
                    ended[:] = [x_in[b], last]
                if b == B - 1:
                    background.append(route(1, b, sets[0], (dve, V), half * HT, HT))
                elif half == 1:
                    background.append(route(1, b, sets[0], (pool, G)))

            UNITS = 2 * BT
            LEAD = 3
            maxima = (step for i in range(NTEAM) for j in range(TEAM) for t in range(BT) for step in row_max(i, j, t))
            STEPS = 2 * TEAM * BT // UNITS

            for _ in prepare(0, (dve, V)):
                pass
            load_operands(0)
            blank_slot(1)
            blank_slot(2)
            load_operands(1)
            for _ in range(2 * TEAM * BT + LEAD * STEPS + 1):
                next(maxima)

            score_free = [None] * 2
            probs_free = [None] * PROBS
            exp_of = {}
            scored = 0
            previous = None

            def value_product(unit):
                i, half, kt, first = unit
                b, team = divmod(i, TEAMS)
                pe.wait(values_ready[b])
                if kt == 0:
                    pe.wait(value_free[0])
                for j in range(TEAM):
                    pe.wait(exp_of[first + j])
                    last = (pe.mark if j == TEAM - 1 else pe.do)(
                        TE.matmul, value_bank[j * VS:j * VS + VW, :], values[:, b % 2, kt, team * TEAM + j, :],
                        probs[:, (first + j) % PROBS, :], start=(kt == 0), stop=(kt == BT - 1))
                for j in range(TEAM):
                    probs_free[(first + j) % PROBS] = last
                values_free[b] = last
                if kt == BT - 1:
                    urgent.append(finish_half(i, half, last))
                    next(urgent[-1])

            def next_job():
                while urgent or background:
                    queue = current[0] if Side.held else urgent or background
                    current[0] = queue
                    try:
                        next(queue[0])
                        return
                    except StopIteration:
                        queue.popleft()

            current = [None]
            STEPS_AFTER = [1, 0, 1, 2]
            assert sum(STEPS_AFTER) == STEPS

            for i in range(NTEAM):
                b, team = divmod(i, TEAMS)
                s = i % SLOTS
                if team == 0 and b + 1 < B:
                    background.append(prepare(b + 1, (pool, G)))
                if i + 2 < NTEAM:
                    if (i + 2) % TEAMS == 0:
                        while (i + 2) // TEAMS not in values_ready:
                            next_job()
                    load_operands(i + 2)
                pe.wait(max_in[i])
                for u in range(UNITS):
                    half, kt = divmod(u, BT)
                    first = scored
                    for j in range(TEAM):
                        n = scored % 2
                        pe.wait(score_free[n])
                        scores = pe.mark(TE.matmul, score_bank[n][:, :], left[0:KROWS, s, j, kt * P:(kt + 1) * P],
                                         right[0:KROWS, s, j, half * HALF:(half + 1) * HALF],
                                         start=True, stop=True)
                        act.wait(scores, probs_free[scored % PROBS])
                        exp_of[scored] = score_free[n] = act.mark(
                            S.activation, probs[:, scored % PROBS, :], score_bank[n][:, :], ACT.Exp, scale=SCALE)
                        scored += 1
                        for _ in range(STEPS_AFTER[j]):
                            next(maxima, None)
                        if j == 1 and previous:
                            value_product(previous)
                        if j != 2:
                            next_job()
                    previous = (i, half, kt, first)
                scores_done[i] = scores
            value_product(previous)
            while urgent or background:
                next_job()
            Side.banks = [0, 1, 2, 3]
            own.close()
            return ended

        x_in_sum_of = {0: x_in_sum}
        routes = deque(route(0, b, sets[b % SETS], (dve, V)) for b in range(B))
        folding = fold_expert_vectors()
        active, rounds = [routes.popleft()], 0
        while active:
            rounds += 1
            next(folding, None)
            if rounds % STAGGER == 0 and rounds < SETS * STAGGER:
                active.append(routes.popleft())
            for job in list(active):
                if next(job, "over") == "over":
                    active.remove(job)
                    if routes and rounds >= SETS * STAGGER:
                        active.append(routes.popleft())
        first.close()
        added = experts(0, [*folded, *Side.free.values(), *wide_free, *rows_written[0]])
        sp.wait(*added)
        for b in range(B):
            x_in[b] = sp.dma(lane_x[b], batch(b), batch_rows(sum_dram[0], b))
        ended = attention(added)
        added = experts(1, ended + [*Side.free.values(), *wide_free])
        sp.wait(*added)
        sp.wait(sp.dma(lane_out, out_rows, sum_dram[1][0:TOKENS, :]))

        block = stack.enter_context(nc.Block())

        @block.sync
        def _(engine):
            sp.play()

        @block.gpsimd
        def _(engine):
            pool.play()

        @block.scalar
        def _(engine):
            act.play()

        @block.vector
        def _(engine):
            dve.play()

        @block.tensor
        def _(engine):
            pe.play()


_INS = ["L0_attn_x", "L0_attn_W_qkv", "L0_attn_W_o", "L0_ffn_ln_g", "L0_ffn_ln_b", "L0_ffn_router_w",
        "L0_ffn_eg", "L0_ffn_eb", "L0_ffn_W1", "L0_ffn_b1", "L0_ffn_W2", "L0_ffn_b2", "L0_ffn_Wo", "L0_ffn_bo"]


def kernel(**inputs):
    import numpy as _np
    import concourse.bacc as _bacc
    from concourse import mybir as _mybir
    from concourse.bass_utils import run_bass_kernel_spmd as _run

    nc = _bacc.Bacc("TRN2", target_bir_lowering=False, num_devices=1)
    arrays, args = {}, []
    for name in _INS:
        a = _np.ascontiguousarray(inputs[name])
        arrays[f"in_{name}"] = a
        args.append(nc.dram_tensor(f"in_{name}", a.shape, _mybir.dt.from_np(a.dtype), kind="ExternalInput").ap())
    x = inputs["L0_attn_x"]
    args.append(nc.dram_tensor("out_x", x.shape, _mybir.dt.from_np(_np.dtype(x.dtype)), kind="ExternalOutput").ap())
    build_macaron(nc, *args)
    r = _run(nc, [arrays], core_ids=[0])
    return r.results[0]["out_x"]
```

```python
import concourse.bass as bass
from concourse import mybir
from contextlib import ExitStack
from collections import deque

F32 = mybir.dt.float32
BF16 = mybir.dt.bfloat16
I32 = mybir.dt.int32
ALU = mybir.AluOpType
ACT = mybir.ActivationFunctionType
AX = mybir.AxisListType


class Token:

    def __init__(self, sem, value):
        self.sem, self.value = sem, value


class Queue:

    def __init__(self, engine, sem):
        self.engine, self.sem, self.count, self.items, self.seen = engine, sem, 0, [], {}

    def wait(self, *tokens):
        for token in tokens:
            if token is not None and self.seen.get(id(token.sem), 0) < token.value:
                self.seen[id(token.sem)] = token.value
                self.items.append((self.engine.wait_ge, (token.sem, token.value), {}, None))

    def do(self, op, /, *args, **kwargs):
        self.items.append((op, args, kwargs, None))

    def mark(self, op, /, *args, **kwargs):
        self.count += 1
        self.items.append((op, args, kwargs, (self.sem, 1)))
        return Token(self.sem, self.count)

    def then(self, op, /, *args, **kwargs):
        token = self.mark(op, *args, **kwargs)
        self.wait(token)
        return token

    def dma(self, lane, out, in_):
        lane.count += 16
        self.items.append((self.engine.dma_start, (out, in_), {}, (lane.sem, 16)))
        return Token(lane.sem, lane.count)

    def counted(self, lane, issue):
        lane.count += 16
        self.items.append((issue, (), {}, (lane.sem, 16)))
        return Token(lane.sem, lane.count)

    def scatter(self, lane, out, rows, in_, **kwargs):
        lane.count += 16
        self.items.append((self.engine.indirect_dma_start,
                           (out, bass.IndirectOffsetOnAxis(ap=rows, axis=0), in_, None), kwargs, (lane.sem, 16)))
        return Token(lane.sem, lane.count)

    def play(self):
        for op, args, kwargs, inc in self.items:
            instruction = op(*args, **kwargs)
            if inc:
                instruction.then_inc(*inc)


class Lane:

    def __init__(self, sem):
        self.sem, self.count = sem, 0


def build_macaron(nc, x, w_qkv, w_o, ln_g, ln_b, router_w, eg, eb, w1, b1, w2, b2, wo, bo, out):
    P = 128
    B, N, F = x.shape
    E, D, H = w1.shape
    HEADS = 16
    DH = F // HEADS
    SCALE = 1.0 / float(DH) ** 0.5
    EPS = 1e-5
    TOPK = 2
    STAGGER = 12
    FOLD_FROM, FOLD_EVERY = 24, 5
    LAG = 2

    HC = H // P
    BT = N // P
    T = B * BT
    TOKENS = B * N
    X2_LIMIT, LIMIT = 20.0, 10000.0

    W1, W2, WO = 0, H, 2 * H
    BIAS1, BIAS2, CLIP_LO, CLIP_HI = (3 * H + k * HC for k in range(4))
    BO = 3 * H + 4 * HC
    RECORD = BO + F

    GATE, NUMBER, ROW = F, F + 1, F + 2
    BLOCK = 2 * P
    BH = BLOCK // P
    REGION = TOKENS + BLOCK
    BLOCKS = (TOPK * TOKENS - E) // BLOCK + E
    SLOTS = 6

    stack = ExitStack()
    with stack:
        def sbuf(name, shape, dt=F32, owner=stack):
            return owner.enter_context(nc.sbuf_tensor(name, shape, dt))

        def semaphore(name):
            return stack.enter_context(nc.semaphore(name))

        pe = Queue(nc.tensor, semaphore("pe_done"))
        act = Queue(nc.scalar, semaphore("act_done"))
        dve = Queue(nc.vector, semaphore("dve_done"))
        pool = Queue(nc.gpsimd, semaphore("pool_done"))
        sp = Queue(nc.sync, semaphore("sp_done"))
        V, G, S, TE = nc.vector, nc.gpsimd, nc.scalar, nc.tensor

        x_sb = sbuf("x_sb", [P, T, F])
        record = sbuf("record", [P, E, RECORD])
        ln_g_bc = sbuf("ln_g_bc", [P, F])
        ln_b_bc = sbuf("ln_b_bc", [P, F])
        router_sb = sbuf("router_sb", [P, E])
        identity = sbuf("identity", [P, P])
        before = sbuf("before", [P, P], BF16)
        ones = sbuf("ones", [P, P], BF16)
        earlier = sbuf("earlier", [P, E, E])
        minus_half = sbuf("minus_half", [P, 1])
        number = sbuf("number", [P, T])
        region = sbuf("region", [P, E])
        block_f = sbuf("block_f", [1, BLOCKS])
        unit = sbuf("unit", [1, E])
        tiles_i = sbuf("tiles_i", [1, E], I32)
        tiles_f = sbuf("tiles_f", [1, E])
        tiles_end = sbuf("tiles_end", [1, E])
        tiles_start = sbuf("tiles_start", [1, E])
        end_f = sbuf("end_f", [1, E])
        end_i = sbuf("end_i", [1, E], I32)
        passed = sbuf("passed", [1, BLOCKS, E + 1])
        within = sbuf("within", [1, BLOCKS, E])
        local = sbuf("local", [1, BLOCKS])
        whose = sbuf("whose", [1, 2, BLOCKS])
        whose_i = sbuf("whose_i", [1, 2, BLOCKS], I32)
        wqkv_t = sbuf("wqkv_t", [P, P])
        wo_t = sbuf("wo_t", [P, P])

        class Set:

            def __init__(self, k, owner):
                def buf(name, shape, dt=F32):
                    return sbuf(f"{name}{k}", shape, dt, owner)

                self.stats = buf("stats", [P, BT, 6])
                self.mean_var = buf("mean_var", [P, BT, 2])
                self.shifted = buf("shifted", [P, BT])
                self.rstd = buf("rstd", [P, BT])
                self.xf = buf("xf", [P, BT, F])
                self.xf_t = buf("xf_t", [P, N])
                self.rows = buf("rows", [P, BT, TOPK, ROW])
                self.logits = buf("logits", [P, BT, E])
                self.ties = buf("ties", [P, BT, E, E])
                self.wins = buf("wins", [P, BT, E, E])
                self.rank = buf("rank", [P, BT, E])
                self.is_top = buf("is_top", [P, TOPK, BT, E])
                self.picked = buf("picked", [P, TOPK, BT, E])
                self.top = buf("top", [P, TOPK, BT])
                self.ratio = buf("ratio", [P, BT])
                self.chosen = buf("chosen", [P, BT, E], BF16)
                self.tallies = buf("tallies", [P, 2, BT, E])
                self.counts = buf("counts", [P, BT + 1, E])
                self.place = buf("place", [P, BT, E])
                self.place_f = buf("place_f", [P, TOPK, BT])
                self.place_i = buf("place_i", [P, TOPK, BT], I32)
                self.scattered = ()
                self.lanes = [Lane(semaphore(f"rows_out{k}_{j}")) for j in range(TOPK)]

        sets = [Set(0, stack)]

        bank = [stack.enter_context(nc.psum_tensor(f"bank{i}", [P, 512], F32)) for i in range(4)]
        wide = [stack.enter_context(nc.psum_tensor(f"wide{i}", [P, 1024], F32)) for i in range(2)]

        rows_dram = [nc.dram_tensor(f"rows{k}_dram", [E * REGION + BLOCK, ROW], F32) for k in range(2)]
        filler_dram = nc.dram_tensor("filler_dram", [BLOCK, ROW], F32)
        sum_dram = [nc.dram_tensor(f"sum{k}_dram", [TOKENS + BLOCK, F], F32) for k in range(2)]

        lane_x = [Lane(semaphore(f"x_in{b}")) for b in range(B)]
        lane_norm = Lane(semaphore("norm_and_router_in"))
        lane_const = Lane(semaphore("const_in"))
        lane_w = [Lane(semaphore(f"expert_in{e}")) for e in range(E)]
        lane_sum = Lane(semaphore("x_into_sum"))
        lane_filler = Lane(semaphore("filler_made"))
        lane_fill = [Lane(semaphore(f"filler_out{k}")) for k in range(2)]
        lane_block = [Lane(semaphore(f"block_in{k}")) for k in range(SLOTS)]
        lane_add = [Lane(semaphore(f"added{k}")) for k in range(BH)]
        lane_out = Lane(semaphore("out_written"))

        wide_free, taken = [None, None], [0]

        def take_wide():
            n = taken[0] % 2
            taken[0] += 1
            pe.wait(wide_free[n])
            return n

        class Side:
            banks, turn, free, held = [0, 1, 2, 3], 0, {}, 0

        def take_bank():
            n = Side.banks[Side.turn % len(Side.banks)]
            Side.turn += 1
            Side.held += 1
            assert Side.free.get(n, None) != "held"
            pe.wait(Side.free.get(n))
            Side.free[n] = "held"
            return n

        def give_bank(n, token):
            Side.held -= 1
            Side.free[n] = token
            return token

        def batch_rows(tensor, b):
            return tensor[b * N:(b + 1) * N, :].rearrange("(p t) f -> p t f", p=P)

        def batch(b):
            return x_sb[:, b * BT:(b + 1) * BT, :]

        first = ExitStack()
        sets.extend(Set(k, first) for k in range(1, B))
        VEC = 2 * E + 2 * E * HC
        vec_rows = sbuf("vec_rows", [VEC, P], owner=first)
        vecs = sbuf("vecs", [P, VEC], owner=first)
        eg_col, eb_col = vecs[:, 0:E], vecs[:, E:2 * E]
        b_col = [vecs[:, 2 * E:2 * E + E * HC], vecs[:, 2 * E + E * HC:VEC]]

        x_rows = x.rearrange("b n f -> (b n) f")
        out_rows = out.rearrange("b n f -> (b n) f")
        x_in = {0: sp.dma(lane_x[0], batch(0), batch_rows(x_rows, 0))}
        sp.dma(lane_norm, ln_g_bc[:, :], ln_g.unsqueeze(0).to_broadcast([P, F]))
        sp.dma(lane_norm, ln_b_bc[:, :], ln_b.unsqueeze(0).to_broadcast([P, F]))
        norm_in = sp.dma(lane_norm, router_sb[:, :], router_w)
        for b in range(1, B):
            x_in[b] = sp.dma(lane_x[b], batch(b), batch_rows(x_rows, b))
        sp.dma(lane_const, vec_rows[0:E, :], eg)
        sp.dma(lane_const, vec_rows[E:2 * E, :], eb)
        sp.dma(lane_const, vec_rows[2 * E:2 * E + E * HC, :], b1.rearrange("e (c p) -> (e c) p", p=P))
        sp.dma(lane_const, vec_rows[2 * E + E * HC:VEC, :], b2.rearrange("e (c p) -> (e c) p", p=P))
        const_in = sp.dma(lane_const, record[:, :, BO:BO + F], bo.unsqueeze(0).to_broadcast([P, E, F]))
        expert_in = []
        for e in range(E):
            sp.dma(lane_w[e], record[:, e, W1:W1 + H], w1[e])
            sp.dma(lane_w[e], record[:, e, W2:W2 + H], w2[e])
            expert_in.append(sp.dma(lane_w[e], record[:, e, WO:WO + H].rearrange("p (c d) -> p c d", d=F),
                                    wo[e].rearrange("(c p) d -> p c d", p=P)))
        x_in_sum = sp.dma(lane_sum, sum_dram[0][0:TOKENS, :], x_rows)

        pool.then(G.memset, identity[:, :], 0.0)
        identity_made = pool.then(G.affine_select, out=identity[:, :], in_=identity[:, :],
                                  compare_op=ALU.not_equal, fill=1.0, base=0,
                                  pattern=[[-1, P]], channel_multiplier=1)
        pool.do(G.memset, minus_half[:, :], -0.5)
        pool.do(G.memset, ones[:, :], 1.0)
        pool.then(G.memset, before[:, :], 1.0)
        pool.do(G.affine_select, out=before[:, :], in_=before[:, :], compare_op=ALU.is_gt, fill=0.0,
                base=0, pattern=[[1, P]], channel_multiplier=-1)
        pool.then(G.memset, earlier[:, :, :], 1.0)
        pool.do(G.affine_select, out=earlier[:, :, :], in_=earlier[:, :, :], compare_op=ALU.is_gt,
                fill=0.0, base=0, pattern=[[1, E], [-1, E]], channel_multiplier=0)
        numbering = sbuf("numbering", [P, T], I32, first)
        regions = sbuf("regions", [P, E], I32, first)
        blocks_i = sbuf("blocks_i", [1, BLOCKS], I32, first)
        spares_i = sbuf("spares_i", [P, BH], I32, first)
        filler = sbuf("filler", [P, BH, ROW], owner=first)
        pool.do(G.iota, numbering[:, :], pattern=[[N, B], [1, BT]], base=0, channel_multiplier=BT)
        pool.do(G.iota, regions[:, :], pattern=[[REGION, E]], base=0, channel_multiplier=0)
        pool.do(G.iota, blocks_i[:, :], pattern=[[1, BLOCKS]], base=0, channel_multiplier=0)
        pool.do(G.iota, spares_i[:, :], pattern=[[1, BH]], base=TOKENS, channel_multiplier=BH)
        pool.do(G.memset, unit[:, :], 1.0)
        counted = pool.mark(G.memset, filler[:, :, :], 0.0)
        dve.wait(counted)
        dve.do(V.tensor_copy, number[:, :], numbering[:, :])
        dve.do(V.tensor_copy, region[:, :], regions[:, :])
        dve.do(V.tensor_copy, block_f[:, :], blocks_i[:, :])
        constants_made = dve.then(V.tensor_copy, filler[:, :, NUMBER], spares_i[:, :])
        sp.wait(constants_made)
        filler_made = sp.dma(lane_filler, filler_dram[:, :].rearrange("(p r) c -> p r c", r=BH), filler[:, :, :])
        sp.wait(filler_made)
        for k in range(2):
            sp.dma(lane_fill[k], rows_dram[k][E * REGION:E * REGION + BLOCK, :], filler_dram[:, :])

        folded = []

        def fold_expert_vectors():
            vec_bank = wide[0][:, 0:VEC]
            bias_bank = [wide[1][:, k * 512:k * 512 + E * HC] for k in range(2)]
            pe.wait(const_in, identity_made)
            turned = pe.mark(TE.transpose, vec_bank, vec_rows[:, :], identity[0:VEC, 0:VEC])
            act.wait(turned)
            copied = wide_free[0] = act.mark(S.copy, vecs[:, :], vec_bank)
            act.wait(copied)
            pe.wait(copied)
            yield
            for e in range(E):
                pe.wait(expert_in[e])
                for k, w in enumerate((W1, W2)):
                    for c in range(HC):
                        last = pe.mark(TE.matmul, bias_bank[k][:, e * HC + c:e * HC + c + 1],
                                       record[:, e, w + c * P:w + (c + 1) * P], eb_col[:, e:e + 1],
                                       start=True, stop=True)
                act.wait(last)
                both = record[:, e, W1:W1 + 2 * H]
                scaled = act.mark(S.activation, both, both, ACT.Copy, scale=eg_col[:, e:e + 1])
                yield
            bias = [record[:, :, at:at + HC] for at in (BIAS1, BIAS2)]
            dve.wait(last, copied)
            for k in range(2):
                wide_free[1] = dve.then(V.tensor_tensor, bias[k], bias_bank[k].rearrange("p (e c) -> p e c", c=HC),
                                        b_col[k].rearrange("p (e c) -> p e c", c=HC), ALU.add)
            dve.do(V.tensor_scalar, record[:, :, CLIP_LO:CLIP_LO + HC], bias[1], -1.0, -X2_LIMIT,
                   ALU.mult, ALU.add)
            folded[:] = [scaled, dve.then(V.tensor_scalar, record[:, :, CLIP_HI:CLIP_HI + HC], bias[1], -1.0,
                                          X2_LIMIT, ALU.mult, ALU.add)]

        def row_statistics(src, nt, r):
            for t in range(nt):
                last = dve.mark(V.bn_stats, out=r.stats[:, t, :], in_=src[:, t, :])
                if t % 2:
                    yield
            dve.wait(last)
            for t in range(nt):
                last = dve.mark(V.bn_aggr, out=r.mean_var[:, t, :], in_=r.stats[:, t, :])
                if t == nt // 2:
                    yield
            dve.wait(last)

        def inverse_deviation(r, nt, scale=1.0, shift=EPS):
            ready = dve.mark(V.tensor_scalar, r.shifted[:, 0:nt], r.mean_var[:, 0:nt, 1], scale, shift,
                             ALU.mult, ALU.add)
            for _ in range(LAG):
                yield
            pool.wait(ready)
            ready = pool.mark(G.tensor_tensor, r.rstd[:, 0:nt], r.shifted[:, 0:nt],
                              minus_half[:, 0:1].to_broadcast([P, nt]), ALU.pow)
            for _ in range(LAG):
                yield
            return ready

        def pause(mill, steps):
            for _ in range(steps if mill[0] is pool else 0):
                yield

        def turn_tiles(dst, tiles, nt, ready):
            for at in range(0, nt, 4):
                n = take_bank()
                pe.wait(ready, identity_made)
                for t in range(4):
                    last = pe.mark(TE.transpose, bank[n][:, t * P:(t + 1) * P], tiles[:, at + t, :],
                                   identity[:, :])
                yield
                act.wait(last)
                turned = give_bank(n, act.mark(S.copy, dst[:, at * P:(at + 4) * P], bank[n][:, :]))
                yield
            return turned

        def route(k_ffn, b, r, mill, t0=0, nt=BT):
            mq, M = mill
            src = x_sb[:, b * BT + t0:b * BT + t0 + nt, :]
            few = slice(0, nt)
            dve.wait(x_in.get(b))
            yield from row_statistics(src, nt, r)
            ready = yield from inverse_deviation(r, nt, 1.0 + EPS, EPS * EPS)
            yield from pause(mill, 2)
            mq.wait(ready)
            for t in range(nt):
                last = mq.mark(M.tensor_scalar, r.xf[:, t, :], src[:, t, :], r.mean_var[:, t, 0:1],
                               r.rstd[:, t:t + 1], ALU.subtract, ALU.mult)
            mq.wait(last)
            yield
            xf = r.xf[:, few, :]
            mq.wait(norm_in)
            mq.then(M.tensor_tensor, xf, xf, ln_g_bc[:, :].unsqueeze(1).to_broadcast([P, nt, F]), ALU.mult)
            yield
            xf_ready = mq.mark(M.tensor_tensor, xf, xf, ln_b_bc[:, :].unsqueeze(1).to_broadcast([P, nt, F]), ALU.add)
            yield from pause(mill, 22)
            yield
            xf_t_ready = yield from turn_tiles(r.xf_t, r.xf, nt, xf_ready)
            n = take_bank()
            pe.wait(xf_t_ready, norm_in)
            for t in range(nt):
                last = pe.mark(TE.matmul, bank[n][:, t * E:(t + 1) * E], r.xf_t[:, t * P:(t + 1) * P],
                               router_sb[:, :], start=True, stop=True)
            yield
            act.wait(last)
            scored = give_bank(n, act.mark(S.copy, r.logits[:, few, :],
                                           bank[n][:, 0:nt * E].rearrange("p (t e) -> p t e", e=E)))
            dve.wait(xf_ready)
            yield from row_statistics(r.xf, nt, r)
            ready = yield from inverse_deviation(r, nt)
            yield from pause(mill, 2)
            shape = [P, nt, E, E]
            theirs = r.logits[:, few, :].unsqueeze(2).to_broadcast(shape)
            mine = r.logits[:, few, :].unsqueeze(3).to_broadcast(shape)
            dve.wait(constants_made, scored)
            dve.do(V.tensor_tensor, r.wins[:, few, :, :], theirs, mine, ALU.is_gt)
            yield
            dve.then(V.tensor_tensor, r.ties[:, few, :, :], theirs, mine, ALU.is_equal)
            yield
            dve.then(V.tensor_tensor, r.ties[:, few, :, :], r.ties[:, few, :, :],
                    earlier[:, :, :].unsqueeze(1).to_broadcast(shape), ALU.mult)
            yield
            dve.then(V.tensor_tensor, r.wins[:, few, :, :], r.wins[:, few, :, :], r.ties[:, few, :, :],
                     ALU.add)
            mq.wait(ready, *r.scattered)
            for t in range(nt):
                filled = mq.mark(M.tensor_scalar, r.rows[:, t, :, 0:F],
                                 r.xf[:, t, :].unsqueeze(1).to_broadcast([P, TOPK, F]),
                                 r.mean_var[:, t, 0:1], r.rstd[:, t:t + 1], ALU.subtract, ALU.mult)
            yield from pause(mill, 14)
            dve.then(V.tensor_reduce, out=r.rank[:, few, :], in_=r.wins[:, few, :, :], axis=AX.X, op=ALU.add)
            yield from pause(mill, 1)
            for k in range(TOPK):
                last = dve.mark(V.tensor_scalar, r.is_top[:, k, few, :], r.rank[:, few, :], float(k), None,
                                ALU.is_equal)
            dve.wait(last)
            chosen_ready = dve.mark(V.tensor_tensor, r.chosen[:, few, :], r.is_top[:, 0, few, :], r.is_top[:, 1, few, :],
                                    ALU.add)
            yield
            n = take_bank()
            pe.wait(chosen_ready)
            flat = r.chosen[:, few, :].rearrange("p t e -> p (t e)")
            pe.do(TE.matmul, bank[n][:, 0:nt * E], before[:, :], flat, start=True, stop=True)
            tallied = pe.mark(TE.matmul, bank[n][:, nt * E:2 * nt * E], ones[:, :], flat, start=True, stop=True)
            yield from pause(mill, 1)
            dve.then(V.tensor_tensor, r.picked[:, :, few, :], r.is_top[:, :, few, :],
                     r.logits[:, few, :].unsqueeze(1).to_broadcast([P, TOPK, nt, E]), ALU.mult)
            dve.then(V.tensor_reduce, out=r.top[:, :, few], in_=r.picked[:, :, few, :], axis=AX.X, op=ALU.add)
            led = dve.mark(V.tensor_tensor, r.ratio[:, few], r.top[:, 1, few], r.top[:, 0, few], ALU.subtract)
            yield
            act.wait(led, tallied)
            shared = act.mark(S.activation, r.ratio[:, few], r.ratio[:, few], ACT.Exp)
            tallies_in = give_bank(n, act.mark(S.copy, r.tallies[:, :, few, :],
                                               bank[n][:, 0:2 * nt * E].rearrange("p (k t e) -> p k t e", k=2, e=E)))
            yield
            total = running[0]
            running[0] = r.counts[:, nt, :]
            dve.wait(tallies_in)
            if total is None:
                dve.then(V.memset, r.counts[:, 0, :], 0.0)
            else:
                dve.then(V.tensor_copy, r.counts[:, 0, :], total)
            for t in range(nt):
                dve.then(V.tensor_tensor, r.counts[:, t + 1, :], r.counts[:, t, :], r.tallies[:, 1, t, :], ALU.add)
                if t % 4 == 3:
                    yield
            yield
            dve.then(V.tensor_tensor, r.place[:, few, :], r.tallies[:, 0, few, :], r.counts[:, few, :], ALU.add)
            dve.then(V.tensor_tensor, r.place[:, few, :], r.place[:, few, :],
                     region[:, :].unsqueeze(1).to_broadcast([P, nt, E]), ALU.add)
            yield from pause(mill, 1)
            dve.then(V.tensor_tensor, r.picked[:, :, few, :], r.is_top[:, :, few, :],
                     r.place[:, few, :].unsqueeze(1).to_broadcast([P, TOPK, nt, E]), ALU.mult)
            dve.then(V.tensor_reduce, out=r.place_f[:, :, few], in_=r.picked[:, :, few, :], axis=AX.X, op=ALU.add)
            dve.wait(*r.scattered)
            dve.do(V.tensor_copy, r.place_i[:, :, few], r.place_f[:, :, few])
            yield
            dve.wait(shared)
            dve.then(V.tensor_scalar, r.top[:, 0, few], r.ratio[:, few], 1.0, None, ALU.add)
            dve.then(V.reciprocal, r.top[:, 1, few], r.top[:, 0, few])
            dve.wait(filled)
            dve.do(V.tensor_scalar, r.rows[:, few, 0, GATE], r.top[:, 1, few], 0.5, None, ALU.mult)
            dve.do(V.scalar_tensor_tensor, r.rows[:, few, 1, GATE], r.top[:, 1, few], 0.5, r.ratio[:, few],
                   ALU.mult, ALU.mult)
            placed = dve.then(V.tensor_copy, r.rows[:, few, :, NUMBER],
                              number[:, b * BT + t0:b * BT + t0 + nt].unsqueeze(2).to_broadcast([P, nt, TOPK]))
            yield
            pool.wait(placed)
            out_now = [None] * TOPK
            for t in range(nt):
                for k in range(TOPK):
                    out_now[k] = pool.scatter(r.lanes[k], rows_dram[k_ffn][:, :], r.place_i[:, k, t:t + 1],
                                              r.rows[:, t, k, :])
                yield
            r.scattered = tuple(out_now)
            rows_written[k_ffn].extend(out_now)

        running = [None]
        rows_written = [[], []]

        def lay_out_blocks(k_ffn):
            total = running[0][0:1, :]
            running[0] = None
            dve.then(V.tensor_tensor, end_f[:, :], total, region[0:1, :], ALU.add)
            placed = dve.then(V.tensor_copy, end_i[:, :], end_f[:, :])
            sp.wait(placed)

            def fill_after(e):
                def issue():
                    row = nc.sync.value_load(end_i[0:1, e:e + 1], min_val=0, max_val=E * REGION)
                    return nc.sync.dma_start(rows_dram[k_ffn][bass.ds(row, BLOCK), :], filler_dram[:, :])
                return issue

            for e in range(E):
                filled = sp.counted(lane_fill[k_ffn], fill_after(e))

            dve.then(V.tensor_scalar, tiles_f[:, :], total, float(BLOCK - 1), None, ALU.add)
            dve.then(V.tensor_copy, tiles_i[:, :], tiles_f[:, :])
            dve.then(V.tensor_scalar, tiles_i[:, :], tiles_i[:, :], BLOCK.bit_length() - 1, None,
                     ALU.logical_shift_right)
            dve.then(V.tensor_copy, tiles_f[:, :], tiles_i[:, :])
            dve.then(V.tensor_tensor_scan, tiles_end[:, :], unit[:, :], tiles_f[:, :], 0.0, ALU.mult, ALU.add)
            dve.then(V.tensor_tensor, tiles_start[:, :], tiles_end[:, :], tiles_f[:, :], ALU.subtract)
            shape = [1, BLOCKS, E]
            blocks = block_f[:, :].unsqueeze(2).to_broadcast(shape)
            dve.do(V.memset, passed[:, :, 0:1], 1.0)
            dve.do(V.tensor_tensor, passed[:, :, 1:E + 1], blocks,
                   tiles_end[:, :].unsqueeze(1).to_broadcast(shape), ALU.is_ge)
            dve.then(V.tensor_tensor, within[:, :, :], blocks,
                     tiles_start[:, :].unsqueeze(1).to_broadcast(shape), ALU.subtract)
            dve.then(V.tensor_reduce, out=whose[:, 0, :], in_=passed[:, :, 1:E + 1], axis=AX.X, op=ALU.add)
            dve.then(V.tensor_tensor, passed[:, :, 0:E], passed[:, :, 0:E], passed[:, :, 1:E + 1], ALU.subtract)
            dve.then(V.tensor_tensor, within[:, :, :], within[:, :, :], passed[:, :, 0:E], ALU.mult)
            dve.then(V.tensor_reduce, out=local[:, :], in_=within[:, :, :], axis=AX.X, op=ALU.add)
            dve.do(V.tensor_scalar, whose[:, 1, :], whose[:, 0, :], float(REGION), None, ALU.mult)
            dve.then(V.tensor_scalar, local[:, :], local[:, :], float(BLOCK), None, ALU.mult)
            dve.do(V.tensor_tensor, whose[:, 1, :], whose[:, 1, :], local[:, :], ALU.add)
            dve.then(V.tensor_scalar, whose[:, 0, :], whose[:, 0, :], float(E - 1), None, ALU.min)
            return filled, dve.then(V.tensor_copy, whose_i[:, :, :], whose[:, :, :])

        def experts(k_ffn, start):
            own = ExitStack()

            def buf(name, shape, dt=F32):
                return sbuf(f"ffn{k_ffn}_{name}", shape, dt, own)

            filled, known = lay_out_blocks(k_ffn)

            for q in (dve, pool, act, pe, sp):
                q.wait(*start)
            rec = buf("rec", [P, SLOTS, RECORD])
            block_rows = buf("block_rows", [P, SLOTS, BH, ROW])
            block_t = buf("block_t", [P, 2, BLOCK])
            x2c = buf("x2c", [P, 2, BLOCK])
            silu = buf("silu", [P, 2, BLOCK])
            hidden = buf("hidden", [P, 2, HC, BLOCK])
            y = buf("y", [P, 2, BH, F])
            number_i = buf("number_i", [P, 2, BH], I32)

            chunk_bank = [bank[0], bank[1], bank[2], wide[0][:, 0:512]]
            y_bank = [bank[3][:, 0:BLOCK], wide[1][:, 0:BLOCK]]
            turn_bank = [wide[0][:, 512:512 + BLOCK], wide[1][:, 512:512 + BLOCK]]
            chunk_free = [None] * 4
            y_free, turn_free = [None, None], [None, None]
            hidden_free, hidden_ready, turned_ready = [None, None], {}, {}
            block_in, slot_free = {}, {}
            block_t_free = [None, None]
            silu_done = {}
            added = {}
            product = {}

            def load_record(i):
                s = i % SLOTS
                sp.wait(known, *folded, *slot_free.get(i - SLOTS, ()))

                def issue():
                    expert = nc.sync.value_load(whose_i[0:1, 0, i:i + 1], min_val=0, max_val=E - 1)
                    return nc.sync.dma_start(rec[:, s, :].unsqueeze(1), record[:, bass.ds(expert, 1), :])

                block_in[i] = sp.counted(lane_block[s], issue)

            def load_rows(i):
                s = i % SLOTS
                sp.wait(filled, *rows_written[k_ffn], *slot_free.get(i - SLOTS, ()))

                def issue():
                    row = nc.sync.value_load(whose_i[0:1, 1, i:i + 1], min_val=0, max_val=E * REGION)
                    return nc.sync.dma_start(block_rows[:, s, :, :],
                                             rows_dram[k_ffn][bass.ds(row, BLOCK), :]
                                             .rearrange("(p r) c -> p r c", r=BH))

                block_in[i] = sp.counted(lane_block[s], issue)

            def turn(i):
                s = i % SLOTS
                pe.wait(block_in[i], turn_free[i % 2])
                for r in range(BH):
                    last = pe.mark(TE.transpose, turn_bank[i % 2][:, r * P:(r + 1) * P],
                                   block_rows[:, s, r, 0:F], identity[:, :])
                act.wait(last, block_t_free[i % 2])
                turned_ready[i] = turn_free[i % 2] = act.mark(S.copy, block_t[:, i % 2, :], turn_bank[i % 2])

            def combine(item):
                i, c, n = item
                s = i % SLOTS
                dve.wait(silu_done[n], hidden_free[i % 2])
                chunk_free[n % 4] = dve.mark(
                    V.scalar_tensor_tensor, hidden[:, i % 2, c, :], chunk_bank[n % 4][:, BLOCK:2 * BLOCK],
                    rec[:, s, BIAS1 + c:BIAS1 + c + 1], silu[:, n % 2, :], ALU.add, ALU.mult)
                if c == HC - 1:
                    dve.wait(chunk_free[n % 4])
                    hidden_ready[i] = dve.mark(V.tensor_scalar, hidden[:, i % 2, :, :], hidden[:, i % 2, :, :],
                                               LIMIT, -LIMIT, ALU.min, ALU.max)

            def second_product(i):
                s = i % SLOTS
                pe.wait(hidden_ready[i], y_free[i % 2])
                for r in range(BH):
                    for c in range(HC):
                        last = (pe.mark if (r, c) == (BH - 1, HC - 1) else pe.do)(
                            TE.matmul, y_bank[i % 2][:, r * F:(r + 1) * F],
                            hidden[:, i % 2, c, r * P:(r + 1) * P], rec[:, s, WO + c * F:WO + (c + 1) * F],
                            start=(c == 0), stop=(c == HC - 1))
                hidden_free[i % 2] = product[i] = last

            def add_block(i):
                s = i % SLOTS
                mine = y[:, i % 2, :, :]
                dve.wait(product[i], *added.get(i - 2, ()))
                y_free[i % 2] = dve.then(
                    V.tensor_tensor, mine, y_bank[i % 2].rearrange("p (r f) -> p r f", f=F),
                    rec[:, s, BO:BO + F].unsqueeze(1).to_broadcast([P, BH, F]), ALU.add)
                dve.then(V.tensor_scalar, mine, mine, LIMIT, -LIMIT, ALU.min, ALU.max)
                clipped = dve.mark(V.tensor_copy, number_i[:, i % 2, :], block_rows[:, s, :, NUMBER])
                act.wait(clipped)
                for r in range(BH):
                    weighed = act.mark(S.activation, mine[:, r, :], mine[:, r, :], ACT.Copy,
                                       scale=block_rows[:, s, r, GATE:GATE + 1])
                slot_free[i] = (weighed, product[i])
                pool.wait(weighed, x_in_sum_of[k_ffn], *added.get(i - 1, ()))
                added[i] = [pool.scatter(lane_add[r], sum_dram[k_ffn][:, :], number_i[:, i % 2, r:r + 1],
                                         mine[:, r, :], compute_op=ALU.add) for r in range(BH)]

            load_record(0)
            load_rows(0)
            for i in range(1, SLOTS):
                load_rows(i)
                load_record(i)
            turn(0)
            waiting, n = None, 0
            for i in range(BLOCKS):
                s = i % SLOTS
                pe.wait(turned_ready[i])
                for c in range(HC):
                    both = chunk_bank[n % 4]
                    pe.wait(chunk_free[n % 4])
                    pe.do(TE.matmul, both[:, 0:BLOCK], rec[:, s, W2 + c * P:W2 + (c + 1) * P],
                          block_t[:, i % 2, :], start=True, stop=True)
                    last = pe.mark(TE.matmul, both[:, BLOCK:2 * BLOCK], rec[:, s, W1 + c * P:W1 + (c + 1) * P],
                                   block_t[:, i % 2, :], start=True, stop=True)
                    dve.wait(last, silu_done.get(n - 2))
                    clipped = dve.mark(V.tensor_scalar, x2c[:, n % 2, :], both[:, 0:BLOCK],
                                       rec[:, s, CLIP_LO + c:CLIP_LO + c + 1],
                                       rec[:, s, CLIP_HI + c:CLIP_HI + c + 1], ALU.max, ALU.min)
                    act.wait(clipped, chunk_free[(n - 2) % 4])
                    silu_done[n] = act.mark(S.activation, silu[:, n % 2, :], x2c[:, n % 2, :], ACT.Silu,
                                            bias=rec[:, s, BIAS2 + c:BIAS2 + c + 1])
                    if waiting:
                        combine(waiting)
                    waiting = (i, c, n)
                    n += 1
                    if c == 0 and i + 1 < BLOCKS:
                        turn(i + 1)
                    if c == HC - 1 and i:
                        second_product(i - 1)
                        add_block(i - 1)
                        if i - 1 + SLOTS < BLOCKS:
                            load_rows(i - 1 + SLOTS)
                            load_record(i - 1 + SLOTS)
                block_t_free[i % 2] = last
            combine(waiting)
            second_product(BLOCKS - 1)
            add_block(BLOCKS - 1)
            own.close()
            return added[BLOCKS - 1] + [chunk_free[(n - 1) % 4], turned_ready[BLOCKS - 1], y_free[0], y_free[1],
                                        product[BLOCKS - 1], Token(dve.sem, dve.count), Token(act.sem, act.count)]

        def attention(start):
            own = ExitStack()

            def buf(name, shape, dt=F32):
                return sbuf(f"att_{name}", shape, dt, own)

            PARTS = 3
            ROWS = DH * PARTS * PARTS
            MROWS = -(-ROWS // 32) * 32
            KROWS = MROWS + PARTS
            TEAM = 4
            TEAMS = HEADS // TEAM
            HALF = N // 2
            HT = HALF // P
            SLOTS = 3
            VS = P // TEAM
            VW = VS // 2
            NTEAM = B * TEAMS

            xh = buf("xh", [P, BT, F])
            q_t = buf("q_t", [P, N])
            rest = xh[:, :, :].rearrange("p t f -> p (t f)")
            attn_t = xh_t = buf("xh_t", [P, N])
            parts = buf("parts", [P, PARTS, N], BF16)
            left = buf("left", [P, SLOTS, TEAM, N], BF16)
            right = buf("right", [P, SLOTS, TEAM, N], BF16)
            values = buf("values", [P, 2, BT, HEADS, VW])
            neg_max = buf("neg_max", [P, 2, 2, TEAM, HT])
            max_rest = buf("max_rest", [TEAM * BT, P])
            max_parts = buf("max_parts", [TEAM * BT, 2, PARTS, P], BF16)
            PROBS = 2 * TEAM
            probs = buf("probs", [P, PROBS, HALF])
            o_t = buf("o_t", [P, 2, HALF])
            inv_sum = buf("inv_sum", [P, HT, TEAM])
            attn = buf("attn", [P, BT, F])
            q_dram = nc.dram_tensor("q_parts_dram", [B, P, PARTS, N], BF16)
            q_copies_dram = nc.dram_tensor("q_copies_dram", [B, PARTS, P, PARTS, N], BF16)
            max_dram = nc.dram_tensor("max_parts_dram", [NTEAM, 2, PARTS, TEAM, HALF], BF16)

            lane_max_out = Lane(semaphore("max_parts_out"))
            lane_q = [Lane(semaphore(f"q_parts_out{k}")) for k in range(2)]
            lane_lr = [Lane(semaphore(f"operands_in{s}")) for s in range(SLOTS)]
            lane_max = [Lane(semaphore(f"max_in{s}")) for s in range(SLOTS)]
            score_bank = [bank[0][:, :], bank[1][:, :]]
            value_bank = bank[3]
            Side.banks, Side.free = [2], {}

            for queue in (dve, act, pool, pe, sp):
                queue.wait(*start)

            w_rows = [o_t[:, 0, 0:P], o_t[:, 0, P:2 * P]]
            lane_wa = Lane(semaphore("attention_weights_in"))
            sp.dma(lane_wa, w_rows[0], w_qkv)
            weights_in = sp.dma(lane_wa, w_rows[1], w_o)
            n = take_wide()
            pe.wait(weights_in)
            pe.do(TE.transpose, wide[n][:, 0:P], w_rows[0], identity[:, :])
            last = pe.mark(TE.transpose, wide[n][:, P:2 * P], w_rows[1], identity[:, :])
            act.wait(last)
            act.do(S.copy, wqkv_t[:, :], wide[n][:, 0:P])
            weights_turned = wide_free[n] = act.mark(S.copy, wo_t[:, :], wide[n][:, P:2 * P])

            blank = [None] * SLOTS

            def blank_slot(s):
                dve.do(V.memset, right[:, s, :, :], 0.0)
                cleared = dve.mark(V.memset, values[:, s, :, :, :], 0.0) if s < 2 else None
                if s < 2:
                    dve.wait(cleared)
                    values_blank[s] = dve.mark(V.memset, values[:, s, :, :, DH:DH + 1], 1.0)
                blank[s] = (Token(dve.sem, dve.count),
                            act.mark(S.copy, left[:, s, :, :].rearrange("p j n -> p (j n)"),
                                     ones[:, 0:1].to_broadcast([P, TEAM * N])))

            values_blank = [None, None]
            blank_slot(0)

            value_bank_blank = dve.mark(V.memset, value_bank[:, :], 0.0)

            q_out, values_ready, values_free = {}, {}, {}

            def prepare(b, mill):
                mq, M = mill
                r = sets[0]
                src = batch(b)
                dve.wait(x_in[b])
                yield from row_statistics(src, BT, r)
                ready = yield from inverse_deviation(r, BT)
                yield
                mq.wait(ready)
                for t in range(BT):
                    normed = mq.mark(M.tensor_scalar, xh[:, t, :], src[:, t, :], r.mean_var[:, t, 0:1],
                                     r.rstd[:, t:t + 1], ALU.subtract, ALU.mult)
                yield from pause(mill, 14)
                turned = yield from turn_tiles(xh_t, xh, BT, normed)
                for h in range(2):
                    half = slice(h * HALF, (h + 1) * HALF)
                    n = take_bank()
                    pe.wait(turned, weights_turned)
                    last = pe.mark(TE.matmul, bank[n][:, :], wqkv_t[:, :], xh_t[:, half], start=True, stop=True)
                    yield
                    act.wait(last)
                    projected = give_bank(n, act.mark(S.copy, q_t[:, half], bank[n][:, :]))
                    yield
                mq.wait(projected, q_out.get((b - 1, 1)))
                mq.then(M.tensor_copy, parts[:, 0, :], q_t[:, :])
                mq.then(M.tensor_tensor, rest, q_t[:, :], parts[:, 0, :], ALU.subtract)
                mq.then(M.tensor_copy, parts[:, 1, :], rest)
                mq.then(M.tensor_tensor, rest, rest, parts[:, 1, :], ALU.subtract)
                split = mq.then(M.tensor_copy, parts[:, 2, :], rest)
                yield from pause(mill, 20)
                sp.wait(split)
                for first, heads in enumerate((slice(0, TEAM * DH), slice(TEAM * DH, P))):
                    lane = lane_q[first]
                    q_out[b, first] = sp.dma(lane, q_dram[b, heads], parts[heads, :, :])
                    for k in range(PARTS):
                        yield from pause(mill, 2)
                        q_out[b, first] = sp.dma(lane, q_copies_dram[b, k, heads],
                                                 parts[heads, k:k + 1, :].to_broadcast([heads.stop - heads.start,
                                                                                         PARTS, N]))
                    if b == 0 and first == 0:
                        load_operands(0)
                yield
                for h in range(2):
                    n = take_bank()
                    pe.wait(projected)
                    for t in range(HT):
                        at = (h * HT + t) * P
                        last = pe.mark(TE.transpose, bank[n][:, t * P:(t + 1) * P], q_t[:, at:at + P],
                                       identity[:, :])
                    yield
                    act.wait(last, values_free.get(b - 2), values_blank[b % 2])
                    kept = values[:, b % 2, h * HT:(h + 1) * HT, :, 0:DH].rearrange("p t h d -> p (t h) d")
                    values_in = give_bank(n, act.mark(S.copy, kept,
                                                      bank[n][:, :].rearrange("p (th d) -> p th d", d=DH)))
                    yield
                values_ready[b] = values_in

            operands_in, scores_done = {}, {}

            def load_operands(i):
                b, team = divmod(i, TEAMS)
                s = i % SLOTS
                sp.wait(q_out[b, min(team, 1)], *blank[s], scores_done.get(i - SLOTS))
                heads = slice(team * TEAM * DH, (team + 1) * TEAM * DH)
                for k in range(PARTS):
                    block = slice(k * DH * PARTS, (k + 1) * DH * PARTS)
                    for side, rows in ((left, q_dram[b, heads]), (right, q_copies_dram[b, k, heads])):
                        operands_in[i] = sp.dma(lane_lr[s], side[block, s, :, :],
                                                rows.rearrange("(h d) j n -> (d j) h n", d=DH))

            def row_max(i, j, t):
                n = take_wide()
                s = i % SLOTS
                pe.wait(operands_in[i])
                for h in range(2):
                    last = (pe.do, pe.mark)[h](
                        TE.matmul, wide[n][:, h * HALF:(h + 1) * HALF], left[0:MROWS, s, j, t * P:(t + 1) * P],
                        right[0:MROWS, s, j, h * HALF:(h + 1) * HALF], start=True, stop=True)
                    if h == 0:
                        yield
                dve.wait(last)
                wide_free[n] = dve.mark(V.tensor_reduce, out=neg_max[:, i % 2, t // HT, j, t % HT:t % HT + 1], in_=wide[n][:, :],
                                        axis=AX.X, op=ALU.max, negate=True)
                if (j, t) == (TEAM - 1, BT - 1):
                    due.append([PLACE_LAG, i, [1] if i == 0 else [0, 1], wide_free[n]])
                elif (i, j, t) == (0, TEAM - 1, HT - 1):
                    due.append([PLACE_LAG, i, [0], wide_free[n]])
                yield

            max_in, max_out, max_split = {}, {}, []

            def place_max(i, halves, reduced):
                n = take_bank()
                s = i % SLOTS
                many = len(halves) * TEAM * HT
                pe.wait(reduced)
                turned = pe.mark(TE.transpose, bank[n][0:many, 0:P],
                                 neg_max[:, i % 2, halves[0]:halves[-1] + 1, :, :].rearrange("p g j t -> p (g j t)"),
                                 identity[:, :])
                yield
                mine, left_over = max_parts[0:many, i % 2, :, :], max_rest[0:many, :]
                act.wait(turned, *max_split)
                copied = give_bank(n, act.mark(S.copy, left_over, bank[n][0:many, 0:P]))
                yield
                dve.wait(copied, max_out.get(i - 2), max_out.get(i))
                for k in range(PARTS):
                    last = dve.then(V.tensor_copy, mine[:, k, :], left_over)
                    if k < PARTS - 1:
                        dve.then(V.tensor_tensor, left_over, left_over, mine[:, k, :], ALU.subtract)
                    if k == 0:
                        yield
                max_split[:] = [last]
                sp.wait(last)
                for at, g in enumerate(halves):
                    max_out[i] = sp.dma(lane_max_out, max_dram[i, g].rearrange("k j (t q) -> (j t) k q", q=P),
                                        max_parts[at * TEAM * HT:(at + 1) * TEAM * HT, i % 2, :, :])
                sp.wait(max_out[i])
                for g in halves:
                    max_in[i, g] = sp.dma(lane_max[s], right[MROWS:KROWS, s, :, g * HALF:(g + 1) * HALF], max_dram[i, g])
                max_in[i, halves[0]] = max_in[i, g]

            due = []

            def next_max():
                next(maxima, None)
                for item in due:
                    item[0] -= 1
                if due and due[0][0] <= 0:
                    placing.append(place_max(*due.pop(0)[1:]))

            placing, urgent, background = deque(), deque(), deque()
            attn_free = [None, None]
            o_free = [None, None]
            value_free = [value_bank_blank]
            ended = []

            def finish_half(i, half, summed):
                b, team = divmod(i, TEAMS)
                act.wait(summed, o_free[half])
                copied = value_free[0] = act.mark(S.copy, o_t[:, half, :], value_bank[:, :])
                yield
                yield
                yield
                n = take_bank()
                pe.wait(copied)
                for t in range(HT):
                    last = pe.mark(TE.transpose, bank[n][:, t * P:(t + 1) * P],
                                   o_t[:, half, t * P:(t + 1) * P], identity[:, :])
                o_free[half] = last
                yield
                o = bank[n][:, 0:HT * P].rearrange("p (t j d) -> p t j d", t=HT, j=TEAM)
                dve.wait(last, attn_free[half])
                dve.then(V.reciprocal, inv_sum[:, :, :], o[:, :, :, DH])
                where = attn[:, half * HT:(half + 1) * HT, team * TEAM * DH:(team + 1) * TEAM * DH]
                placed = give_bank(n, dve.then(
                    V.tensor_tensor, where.rearrange("p t (j d) -> p t j d", j=TEAM), o[:, :, :, 0:DH],
                    inv_sum[:, :, :].unsqueeze(3).to_broadcast([P, HT, TEAM, DH]), ALU.mult))
                if team == TEAMS - 1:
                    urgent.append(finish_rows(b, half, placed))

            def finish_rows(b, half, placed):
                r = slice(half * HT, (half + 1) * HT)
                turned = yield from turn_tiles(attn_t[:, half * HALF:(half + 1) * HALF], attn[:, r, :], HT, placed)
                attn_free[half] = turned
                n = take_bank()
                pe.wait(turned)
                for t in range(HT):
                    at = (half * HT + t) * P
                    last = pe.mark(TE.matmul, bank[n][:, t * P:(t + 1) * P], attn_t[:, at:at + P],
                                   wo_t[:, :], start=True, stop=True)
                yield
                rows = batch(b)[:, r, :]
                dve.wait(last)
                x_in[b] = give_bank(n, dve.then(V.tensor_tensor, rows, rows,
                                                bank[n][:, :].rearrange("p (t f) -> p t f", f=F), ALU.add))
                if half == 1:
                    yield
                    sp.wait(x_in[b])
                    x_in_sum_of[1] = sp.dma(lane_sum, batch_rows(sum_dram[1], b), batch(b))
                    ended[:] = [x_in[b], last]
                if b == B - 1:
                    background.append(route(1, b, sets[0], (dve, V), half * HT, HT))
                elif half == 1:
                    background.append(route(1, b, sets[0], (pool, G)))

            UNITS = 2 * BT
            LEAD = 4
            PLACE_LAG = 2
            maxima = (step for i in range(NTEAM) for g in range(2) for j in range(TEAM)
                      for t in range(g * HT, (g + 1) * HT) for step in row_max(i, j, t))
            STEPS = 2 * TEAM * BT // UNITS

            for _ in prepare(0, (dve, V)):
                pass
            blank_slot(1)
            blank_slot(2)
            load_operands(1)
            done = TEAM * BT + PLACE_LAG + 1
            for _ in range(done):
                next_max()
                for _ in placing.popleft() if placing else ():
                    pass

            score_free, n = [None] * 2, 0
            probs_free = [None] * PROBS
            exp_of = {}
            scored = 0
            previous = None

            def value_product(unit):
                i, half, kt, first = unit
                b, team = divmod(i, TEAMS)
                pe.wait(values_ready[b])
                if kt == 0:
                    pe.wait(value_free[0])
                for j in range(TEAM):
                    pe.wait(exp_of[first + j])
                    last = (pe.mark if j == TEAM - 1 else pe.do)(
                        TE.matmul, value_bank[j * VS:j * VS + VW, :], values[:, b % 2, kt, team * TEAM + j, :],
                        probs[:, (first + j) % PROBS, :], start=(kt == 0), stop=(kt == BT - 1))
                for j in range(TEAM):
                    probs_free[(first + j) % PROBS] = last
                values_free[b] = last
                if kt == BT - 1:
                    urgent.append(finish_half(i, half, last))
                    next(urgent[-1])

            def next_job():
                while placing or urgent or background:
                    queue = current[0] if Side.held else placing or urgent or background
                    current[0] = queue
                    try:
                        next(queue[0])
                        return
                    except StopIteration:
                        queue.popleft()

            current = [None]
            STEPS_AFTER = [1, 0, 1, 2]
            assert sum(STEPS_AFTER) == STEPS

            for i in range(NTEAM):
                b, team = divmod(i, TEAMS)
                s = i % SLOTS
                if team == 0 and b + 1 < B:
                    background.append(prepare(b + 1, (pool, G)))
                if i + 2 < NTEAM:
                    if (i + 2) % TEAMS == 0:
                        while (i + 2) // TEAMS not in values_ready:
                            next_job()
                    load_operands(i + 2)
                for u in range(UNITS):
                    half, kt = divmod(u, BT)
                    if kt == 0:
                        pe.wait(max_in[i, half])
                    behind = done < 2 * TEAM * BT + 1 + (LEAD + i * UNITS + u) * STEPS
                    first = scored
                    for j in range(TEAM):
                        if done > 2 * NTEAM * TEAM * BT + PLACE_LAG and len(score_bank) == 2:
                            score_bank += [piece[:, h * HALF:(h + 1) * HALF] for piece in wide for h in range(2)]
                            score_free += [wide_free[0]] * 2 + [wide_free[1]] * 2
                        n = (n + 1) % len(score_bank)
                        pe.wait(score_free[n])
                        scores = pe.mark(TE.matmul, score_bank[n], left[0:KROWS, s, j, kt * P:(kt + 1) * P],
                                         right[0:KROWS, s, j, half * HALF:(half + 1) * HALF],
                                         start=True, stop=True)
                        act.wait(scores, probs_free[scored % PROBS])
                        exp_of[scored] = score_free[n] = act.mark(
                            S.activation, probs[:, scored % PROBS, :], score_bank[n], ACT.Exp, scale=SCALE)
                        scored += 1
                        for _ in range(2 if behind else STEPS_AFTER[j]):
                            next_max()
                            done += 1
                        if j == 1 and previous:
                            value_product(previous)
                        for _ in range((j != 2) * (1 if i < NTEAM - 1 else 2)):
                            next_job()
                    previous = (i, half, kt, first)
                scores_done[i] = scores
            value_product(previous)
            while placing or urgent or background:
                next_job()
            Side.banks = [0, 1, 2, 3]
            wide_free[:] = [score_free[-1], score_free[-1]]
            own.close()
            return ended

        x_in_sum_of = {0: x_in_sum}
        folding = fold_expert_vectors()
        active = {b: route(0, b, sets[b], (dve, V)) for b in range(B)}
        rounds = 0
        while active:
            rounds += 1
            if rounds >= FOLD_FROM and rounds % FOLD_EVERY == 0:
                next(folding, None)
            for b, job in list(active.items()):
                if rounds >= b * STAGGER and next(job, "over") == "over":
                    del active[b]
        for _ in folding:
            pass
        first.close()
        added = experts(0, [*folded, *Side.free.values(), *wide_free, *rows_written[0]])
        sp.wait(*added)
        for b in range(B):
            x_in[b] = sp.dma(lane_x[b], batch(b), batch_rows(sum_dram[0], b))
        ended = attention(added)
        added = experts(1, ended + [*Side.free.values(), *wide_free])
        sp.wait(*added)
        sp.wait(sp.dma(lane_out, out_rows, sum_dram[1][0:TOKENS, :]))

        block = stack.enter_context(nc.Block())

        @block.sync
        def _(engine):
            sp.play()

        @block.gpsimd
        def _(engine):
            pool.play()

        @block.scalar
        def _(engine):
            act.play()

        @block.vector
        def _(engine):
            dve.play()

        @block.tensor
        def _(engine):
            pe.play()


_INS = ["L0_attn_x", "L0_attn_W_qkv", "L0_attn_W_o", "L0_ffn_ln_g", "L0_ffn_ln_b", "L0_ffn_router_w",
        "L0_ffn_eg", "L0_ffn_eb", "L0_ffn_W1", "L0_ffn_b1", "L0_ffn_W2", "L0_ffn_b2", "L0_ffn_Wo", "L0_ffn_bo"]


def kernel(**inputs):
    import numpy as _np
    import concourse.bacc as _bacc
    from concourse import mybir as _mybir
    from concourse.bass_utils import run_bass_kernel_spmd as _run

    nc = _bacc.Bacc("TRN2", target_bir_lowering=False, num_devices=1)
    arrays, args = {}, []
    for name in _INS:
        a = _np.ascontiguousarray(inputs[name])
        arrays[f"in_{name}"] = a
        args.append(nc.dram_tensor(f"in_{name}", a.shape, _mybir.dt.from_np(a.dtype), kind="ExternalInput").ap())
    x = inputs["L0_attn_x"]
    args.append(nc.dram_tensor("out_x", x.shape, _mybir.dt.from_np(_np.dtype(x.dtype)), kind="ExternalOutput").ap())
    build_macaron(nc, *args)
    r = _run(nc, [arrays], core_ids=[0])
    return r.results[0]["out_x"]
```
